# Optimizing a Trainium2 kernel written in Bass

```python
import numpy as np
import jax
import jax.numpy as jnp

def _softmax(x, axis=-1):
    return jax.nn.softmax(x, axis=axis)

def _gelu(x):
    return jax.nn.gelu(x, approximate=True)

def _silu(x):
    return jax.nn.silu(x)

def _sigmoid(x):
    return jax.nn.sigmoid(x)

def _layernorm(x, axis=-1, eps=1e-05):
    m = jnp.mean(x, axis=axis, keepdims=True)
    v = jnp.var(x, axis=axis, keepdims=True)
    return (x - m) / jnp.sqrt(v + eps)

def _scatter_add(tgt, idx, src, axis=0):
    return tgt.at[idx].add(src)

def _segment_sum(src, seg, n):
    return jax.ops.segment_sum(src, seg, n)
kernel_name = 'mk_xattn_seq_d1_seqx_r8_1d617c'

def setup_inputs(seed: int=0):
    np.random.seed(seed)
    _w = jnp.asarray

    def _rec_inputs():
        import jax
        import jax.numpy as jnp
        _rk = jax.random.key(seed)
        x = -0.0002928 + 1 * jax.random.normal(jax.random.fold_in(_rk, 1), (64, 64, 256), jnp.float32)
        _lenS = 64 - jax.random.randint(jax.random.fold_in(_rk, 7), (64,), 0, max(1, 64 // 4) + 1, jnp.int32)
        _lenS2 = 64 - jax.random.randint(jax.random.fold_in(_rk, 8), (64,), 0, max(1, 64 // 4) + 1, jnp.int32)
        _ctx_2048P = jax.random.normal(jax.random.fold_in(_rk, 11), (64, 16, 256), jnp.float32)
        _ctx_2048c = jax.random.dirichlet(jax.random.fold_in(_rk, 511), 0.3 * jnp.ones((16,), jnp.float32), (64, 64))
        _ctx_2048t = jnp.einsum('bsk,bkd->bsd', _ctx_2048c, _ctx_2048P)
        _ctx_2048t = _ctx_2048t * jax.lax.rsqrt(jnp.mean(jnp.square(_ctx_2048t)) + 1e-12) * 0.953939
        ctx_2048 = 0.000189249 + 0.0999589 * (_ctx_2048t + 0.3 * jax.random.normal(jax.random.fold_in(_rk, 611), (64, 64, 256), jnp.float32))
        return (x, ctx_2048)
    x, ctx_2048 = _rec_inputs()

    def _L0_xattn_setup():
        import jax, jax.numpy as jnp
        import numpy as np
        B, L, E, H = (4, 64, 256, 32)
        S = E // H
        EXTRA_MAA, EXTRA_DECAY = (32, 64)
        EPS = 1e-05

        def _ln(x, w, b):
            m = jnp.mean(x, axis=-1, keepdims=True)
            v = jnp.mean((x - m) ** 2, axis=-1, keepdims=True)
            return (x - m) * jax.lax.rsqrt(v + EPS) * w + b

        def _token_shift(xn, prev_row):
            first = (prev_row - xn[:, 0])[:, None]
            rest = xn[:, :-1] - xn[:, 1:]
            return jnp.concatenate([first, rest], axis=1)
        key = jax.random.key(seed)
        ks = jax.random.split(key, 24)
        rn = lambda k, shp, s=1.0: jax.random.normal(k, shp, dtype=jnp.float32) * s
        return dict(x=rn(ks[0], (B, L, E)), state=rn(ks[1], (B, 2 + S, E), 0.1), ln1_w=jnp.ones((E,), jnp.float32), ln1_b=jnp.zeros((E,), jnp.float32), ln2_w=jnp.ones((E,), jnp.float32), ln2_b=jnp.zeros((E,), jnp.float32), maa_x=rn(ks[2], (E,), 0.02), maa_w1=rn(ks[3], (E, 5 * EXTRA_MAA), 0.02), maa_w2=rn(ks[4], (5, EXTRA_MAA, E), 0.02), maa_stack=rn(ks[5], (5, E), 0.02), time_decay=rn(ks[6], (E,), 0.5), decay_w1=rn(ks[7], (E, EXTRA_DECAY), 0.02), decay_w2=rn(ks[8], (EXTRA_DECAY, E), 0.02), faaaa=rn(ks[9], (H, S), 0.1), Wr=rn(ks[10], (E, E), 0.02), Wk=rn(ks[11], (E, E), 0.02), Wv=rn(ks[12], (E, E), 0.02), Wg=rn(ks[13], (E, E), 0.02), Wo=rn(ks[14], (E, E), 0.02), gn_w=jnp.ones((E,), jnp.float32), gn_b=jnp.zeros((E,), jnp.float32), ffn_maa_k=rn(ks[15], (E,), 0.02), ffn_maa_r=rn(ks[16], (E,), 0.02), ffn_Wk=rn(ks[17], (E, E), 0.02), ffn_Wr=rn(ks[18], (E, E), 0.02), ffn_Wv=rn(ks[19], (E, E), 0.02), i=0)
    _L0_xattn_all = _L0_xattn_setup()
    _L0_xattn_in = {k: v for k, v in _L0_xattn_all.items() if k in ('ln1_w', 'ln1_b', 'ln2_w', 'ln2_b', 'maa_x', 'maa_w1', 'maa_w2', 'maa_stack', 'time_decay', 'decay_w1', 'decay_w2', 'faaaa', 'Wr', 'Wk', 'Wv', 'Wg', 'Wo', 'gn_w', 'gn_b', 'ffn_maa_k', 'ffn_maa_r', 'ffn_Wk', 'ffn_Wr', 'ffn_Wv')}
    del _L0_xattn_all
    return {'x': x, 'ctx_2048': ctx_2048, 'L0_xattn_ln1_w': _L0_xattn_in['ln1_w'], 'L0_xattn_ln1_b': _L0_xattn_in['ln1_b'], 'L0_xattn_ln2_w': _L0_xattn_in['ln2_w'], 'L0_xattn_ln2_b': _L0_xattn_in['ln2_b'], 'L0_xattn_maa_x': _L0_xattn_in['maa_x'], 'L0_xattn_maa_w1': _L0_xattn_in['maa_w1'], 'L0_xattn_maa_w2': _L0_xattn_in['maa_w2'], 'L0_xattn_maa_stack': _L0_xattn_in['maa_stack'], 'L0_xattn_time_decay': _L0_xattn_in['time_decay'], 'L0_xattn_decay_w1': _L0_xattn_in['decay_w1'], 'L0_xattn_decay_w2': _L0_xattn_in['decay_w2'], 'L0_xattn_faaaa': _L0_xattn_in['faaaa'], 'L0_xattn_Wr': _L0_xattn_in['Wr'], 'L0_xattn_Wk': _L0_xattn_in['Wk'], 'L0_xattn_Wv': _L0_xattn_in['Wv'], 'L0_xattn_Wg': _L0_xattn_in['Wg'], 'L0_xattn_Wo': _L0_xattn_in['Wo'], 'L0_xattn_gn_w': _L0_xattn_in['gn_w'], 'L0_xattn_gn_b': _L0_xattn_in['gn_b'], 'L0_xattn_ffn_maa_k': _L0_xattn_in['ffn_maa_k'], 'L0_xattn_ffn_maa_r': _L0_xattn_in['ffn_maa_r'], 'L0_xattn_ffn_Wk': _L0_xattn_in['ffn_Wk'], 'L0_xattn_ffn_Wr': _L0_xattn_in['ffn_Wr'], 'L0_xattn_ffn_Wv': _L0_xattn_in['ffn_Wv']}

def reference(x, ctx_2048, L0_xattn_ln1_w, L0_xattn_ln1_b, L0_xattn_ln2_w, L0_xattn_ln2_b, L0_xattn_maa_x, L0_xattn_maa_w1, L0_xattn_maa_w2, L0_xattn_maa_stack, L0_xattn_time_decay, L0_xattn_decay_w1, L0_xattn_decay_w2, L0_xattn_faaaa, L0_xattn_Wr, L0_xattn_Wk, L0_xattn_Wv, L0_xattn_Wg, L0_xattn_Wo, L0_xattn_gn_w, L0_xattn_gn_b, L0_xattn_ffn_maa_k, L0_xattn_ffn_maa_r, L0_xattn_ffn_Wk, L0_xattn_ffn_Wr, L0_xattn_ffn_Wv):
    import jax
    import jax.numpy as jnp

    def _L0_xattn_ref(x, state, ln1_w, ln1_b, ln2_w, ln2_b, maa_x, maa_w1, maa_w2, maa_stack, time_decay, decay_w1, decay_w2, faaaa, Wr, Wk, Wv, Wg, Wo, gn_w, gn_b, ffn_maa_k, ffn_maa_r, ffn_Wk, ffn_Wr, ffn_Wv, i):
        import jax, jax.numpy as jnp
        import numpy as np
        B, L, E, H = (4, 64, 256, 32)
        S = E // H
        EXTRA_MAA, EXTRA_DECAY = (32, 64)
        EPS = 1e-05

        def _ln(x, w, b):
            m = jnp.mean(x, axis=-1, keepdims=True)
            v = jnp.mean((x - m) ** 2, axis=-1, keepdims=True)
            return (x - m) * jax.lax.rsqrt(v + EPS) * w + b

        def _token_shift(xn, prev_row):
            first = (prev_row - xn[:, 0])[:, None]
            rest = xn[:, :-1] - xn[:, 1:]
            return jnp.concatenate([first, rest], axis=1)
        b, l = (x.shape[0], x.shape[1])
        i0 = (2 + S) * i + 0
        i1 = (2 + S) * i + 1
        xn = _ln(x, ln1_w, ln1_b)
        sx = _token_shift(xn, state[:, i1])
        xxx = jnp.tanh((xn + sx * maa_x) @ maa_w1).reshape(b, l, 5, 1, EXTRA_MAA)
        xxx = jnp.matmul(xxx, maa_w2).reshape(b, l, 5, E)
        x5 = xn[:, :, None] + sx[:, :, None] * (maa_stack + xxx)
        w = jnp.exp(-jnp.exp(time_decay + jnp.tanh(x5[:, :, 1] @ decay_w1) @ decay_w2))
        w = w.reshape(b, l, H, S)
        r = (x5[:, :, 3] @ Wr.T).reshape(b, l, H, S)
        k = (x5[:, :, 0] @ Wk.T).reshape(b, l, H, S)
        v = (x5[:, :, 2] @ Wv.T).reshape(b, l, H, S)
        g = jax.nn.silu(x5[:, :, 4] @ Wg.T)
        s0 = state[:, (2 + S) * i + 2:(2 + S) * (i + 1)].reshape(b, H, S, S)
        u = faaaa[None, :, :, None]

        def step(s, rkvw):
            r_t, k_t, v_t, w_t = rkvw
            a = k_t[:, :, :, None] * v_t[:, :, None, :]
            out = jnp.einsum('bhk,bhkd->bhd', r_t, u * a + s)
            return (a + w_t[:, :, :, None] * s, out)
        xs = tuple((jnp.moveaxis(t, 1, 0) for t in (r, k, v, w)))
        _, outs = jax.lax.scan(step, s0, xs)
        att = jnp.moveaxis(outs, 0, 1).reshape(b, l, E)
        a4 = att.reshape(b, l, H, S)
        m = jnp.mean(a4, axis=-1, keepdims=True)
        var = jnp.mean((a4 - m) ** 2, axis=-1, keepdims=True)
        att = ((a4 - m) * jax.lax.rsqrt(var + EPS)).reshape(b, l, E) * gn_w + gn_b
        x = x + att * g @ Wo.T
        xn2 = _ln(x, ln2_w, ln2_b)
        sx2 = _token_shift(xn2, state[:, i0])
        xk = xn2 + sx2 * ffn_maa_k
        xr = xn2 + sx2 * ffn_maa_r
        rr = jax.nn.sigmoid(xr @ ffn_Wr.T)
        kk = jnp.square(jax.nn.relu(xk @ ffn_Wk.T))
        x = x + rr * (kk @ ffn_Wv.T)
        return x
    x = _L0_xattn_ref(x, ctx_2048, L0_xattn_ln1_w, L0_xattn_ln1_b, L0_xattn_ln2_w, L0_xattn_ln2_b, L0_xattn_maa_x, L0_xattn_maa_w1, L0_xattn_maa_w2, L0_xattn_maa_stack, L0_xattn_time_decay, L0_xattn_decay_w1, L0_xattn_decay_w2, L0_xattn_faaaa, L0_xattn_Wr, L0_xattn_Wk, L0_xattn_Wv, L0_xattn_Wg, L0_xattn_Wo, L0_xattn_gn_w, L0_xattn_gn_b, L0_xattn_ffn_maa_k, L0_xattn_ffn_maa_r, L0_xattn_ffn_Wk, L0_xattn_ffn_Wr, L0_xattn_ffn_Wv, 0)
    return x

_drawn_inputs = setup_inputs


def setup_inputs(seed=0):
    import zlib

    import numpy as np

    out = dict(_drawn_inputs(seed))
    spreads = {'L0_xattn_ln1_w': (1.0, 0.561),
     'L0_xattn_ln1_b': (0.0, 0.562),
     'L0_xattn_ln2_w': (1.0, 0.6),
     'L0_xattn_ln2_b': (0.0, 0.8),
     'L0_xattn_gn_w': (1.0, 0.6),
     'L0_xattn_gn_b': (0.0, 0.8)}
    factors = {'ctx_2048': 6.391,
     'L0_xattn_maa_x': 8.0,
     'L0_xattn_maa_w1': 6.979,
     'L0_xattn_maa_w2': 6.961,
     'L0_xattn_maa_stack': 8.0,
     'L0_xattn_time_decay': 2.778,
     'L0_xattn_decay_w1': 8.0,
     'L0_xattn_decay_w2': 8.0,
     'L0_xattn_faaaa': 5.393,
     'L0_xattn_ffn_maa_k': 8.0,
     'L0_xattn_ffn_maa_r': 8.0,
     'L0_xattn_ffn_Wk': 3.049,
     'L0_xattn_ffn_Wr': 8.0,
     'L0_xattn_ffn_Wv': 2.824}
    for name, (base, spread) in spreads.items():
        noise = np.random.default_rng([zlib.crc32(name.encode()), seed]).standard_normal(out[name].shape)
        drawn = base * np.exp(spread * noise) if base else spread * noise
        out[name] = jnp.asarray(drawn.astype(out[name].dtype))
    for name, factor in factors.items():
        out[name] = (out[name] * factor).astype(out[name].dtype)
    return out
```

```python
from contextlib import ExitStack

import concourse.bass as bass
from concourse import mybir

F32 = mybir.dt.float32
ALU = mybir.AluOpType
ACT = mybir.ActivationFunctionType

B, L, E, H = 64, 64, 256, 32
S = E // H
LORA, DECAY = 32, 64
EPS = 1e-5
P = 128
HF = E // P
NB = 8
T = NB * L
NCH = B // NB
TT = T // P
G4 = P // H
JH = S // G4
NQ = JH * HF

VECS = ["ln1_w", "ln1_b", "ln2_w", "ln2_b", "maa_x", "maa0", "maa1", "maa2", "maa3", "maa4",
        "time_decay", "u", "gn_w", "gn_b", "ffn_k", "ffn_r"]
COL = {name: HF * n for n, name in enumerate(VECS)}
MIX_K, MIX_W, MIX_V, MIX_R, MIX_G = range(5)
MIXES = [MIX_V, MIX_K, MIX_W, MIX_R, MIX_G]
LARGE = ["Wr", "Wk", "Wv", "Wg", "Wo", "Fk", "Fr", "Fv"]


def build(nc, x, prev, s0, vecs, w1, w2, dw1, dw2, large, consts, out):
    vscr = nc.dram_tensor("v_scratch", [2, H, S, T], F32, kind="Internal").ap()
    with ExitStack() as ctx:
        def sb(name, shape):
            return ctx.enter_context(nc.sbuf_tensor(name, shape, F32))

        def sem(name):
            return ctx.enter_context(nc.semaphore(name))

        prev_sb = sb("prev_sb", [P, 2, HF, B])
        s0_sb = sb("s0_sb", [P, HF, S, B])
        vec_sb = sb("vec_sb", [P, HF * len(VECS)])
        w1_sb = sb("w1_sb", [P, HF, 2 * P])
        w2_sb = sb("w2_sb", [P, 5, E])
        dw1_sb = sb("dw1_sb", [P, HF, P])
        dw2_sb = sb("dw2_sb", [P, E])
        large_sb = sb("large_sb", [P, len(LARGE), HF, E])
        const_sb = sb("const_sb", [P, 2 * P + HF * P + HF * H])
        gn_half = sb("gn_half", [P, 2 * HF])
        eps_sb = sb("eps_sb", [P, 1])
        neg_half = sb("neg_half", [P, TT])
        ident = const_sb[:, 0:P]
        head_mean = const_sb[:, P:2 * P]
        sum_k_wide = const_sb[:, 2 * P:2 * P + HF * P].rearrange("p (a m) -> p a m", a=HF)
        sum_k = const_sb[:, 2 * P + HF * P:].rearrange("p (a m) -> p a m", a=HF)

        x_tok = sb("x_tok", [P, 2, TT, E])
        st1 = sb("st1", [P, TT, 6])
        mv1 = sb("mv1", [P, TT, 2])
        rs1 = sb("rs1", [P, TT])
        xhat = sb("xhat", [P, TT, E])
        xnp = sb("xnp", [P, HF * NB, L + 1])
        sx = sb("sx", [P, HF, T])
        mix = sb("mix", [P, HF, T])
        th = sb("th", [P, 2, T])
        x5 = sb("x5", [P, 2, HF, T])
        v_sb = sb("v_sb", [P, JH, T])
        k_sb = sb("k_sb", [P, 2, HF, T])
        r_sb = sb("r_sb", [P, 2, HF, T])
        w_sb = sb("w_sb", [P, 2, HF, NB, L])
        thd = sb("thd", [P, T])
        rk = sb("rk", [P, HF, T])
        sg = sb("sg", [P, 2, JH, T])
        bonus = sb("bonus", [P, 2, JH, T])
        vrep = sb("vrep", [P, HF, S, T])
        kv = sb("kv", [P, 2, G4, NB, L])
        att = sb("att", [P, JH, T])
        sq = sb("sq", [P, JH, T])
        rstd = sb("rstd", [P, T])
        xres = sb("xres", [P, TT, E])
        st2 = sb("st2", [P, TT, 6])
        mv2 = sb("mv2", [P, TT, 2])
        rs2 = sb("rs2", [P, TT])
        xn2p = sb("xn2p", [P, HF * NB, L + 1])
        xk = sb("xk", [P, HF, T])
        xr = sb("xr", [P, HF, T])
        trr = sb("trr", [P, TT, E])
        ob = sb("ob", [P, TT, E])

        pa = ctx.enter_context(nc.psum_tensor("pa", [P, 2, T], F32))
        pb = ctx.enter_context(nc.psum_tensor("pb", [P, 2, T], F32))
        pc = ctx.enter_context(nc.psum_tensor("pc", [P, 2, T], F32))
        patt = ctx.enter_context(nc.psum_tensor("patt", [P, JH, T], F32))
        pc_tok = pc[:, :, :].rearrange("p a (t e) -> p (a t) e", e=E)

        in_small, in_w, in_large = sem("in_small"), sem("in_w"), sem("in_large")
        x_in = [sem("x_in0"), sem("x_in1")]
        res_in, v_stored, v_in, out_stored = sem("res_in"), sem("v_stored"), sem("v_in"), sem("out_stored")
        inited, halved, prev1_put, prev2_put, s0_put = [sem(n) for n in ("inited", "halved", "prev1_put", "prev2_put", "s0_put")]
        eps1_added, rstd1_ready, eps2_added, rstd2_ready = [sem(n) for n in ("eps1_added", "rstd1_ready", "eps2_added", "rstd2_ready")]
        st1_ready, mv1_ready, xhat_ready, sx_ready, mix_ready = [sem(n) for n in ("st1_ready", "mv1_ready", "xhat_ready", "sx_ready", "mix_ready")]
        mixed, x5_ready, rk_ready, bonus_ready, sg_ready = [sem(n) for n in ("mixed", "x5_ready", "rk_ready", "bonus_ready", "sg_ready")]
        kv_ready, state_ready, rs_ready = [sem(n) for n in ("kv_ready", "state_ready", "rs_ready")]
        att_ready, cen_ready, scaled, y_ready, x2_ready = [sem(n) for n in ("att_ready", "cen_ready", "scaled", "y_ready", "x2_ready")]
        st2_ready, mv2_ready, xhat2_ready, sx2_ready, xk_ready, xr_ready = [sem(n) for n in ("st2_ready", "mv2_ready", "xhat2_ready", "sx2_ready", "xk_ready", "xr_ready")]
        gated, out_ready = sem("gated"), sem("out_ready")
        xn_ready, th_ready, v_ready, k_ready, thd_ready, r_ready = [sem(n) for n in ("xn_ready", "th_ready", "v_ready", "k_ready", "thd_ready", "r_ready")]
        e_ready, w_ready, tg_ready, sq_ready, ln_ready, rstd_ready = [sem(n) for n in ("e_ready", "w_ready", "tg_ready", "sq_ready", "ln_ready", "rstd_ready")]
        xn2_ready, trr_ready, relu_ready, kk_ready = [sem(n) for n in ("xn2_ready", "trr_ready", "relu_ready", "kk_ready")]
        t1_done, w1_done, x_done, pv_done, pk_done, d1_done, pr_done, d2_done, pg_done, cb_done = [
            sem(n) for n in ("t1_done", "w1_done", "x_done", "pv_done", "pk_done", "d1_done", "pr_done", "d2_done", "pg_done", "cb_done")]
        summed, mean_done, var_done, wo_done, t2_done, rr_done, kk_done, y2_done = [
            sem(n) for n in ("summed", "mean_done", "var_done", "wo_done", "t2_done", "rr_done", "kk_done", "y2_done")]

        tg = sb("tg", [P, JH, T])
        e_buf, kk_buf, xhat2, sx2 = tg, sq, ob, rk

        def vec(name, half):
            return vec_sb[:, COL[name] + half:COL[name] + half + 1]

        def weight(name, kt):
            return large_sb[:, LARGE.index(name), kt, :]

        def by_seq(ap):
            return ap.rearrange("p (b t) -> p b t", b=NB)

        v_in_half = [v_in, sem("v_in1")]

        def x5_slot(n):
            return n % 2

        block = ctx.enter_context(nc.Block())

        @block.sync
        def _(sp):
            def load_x(c, p):
                if c >= 2:
                    sp.wait_ge(xhat_ready, TT * (c - 1))
                sp.dma_start(x_tok[:, p], x[c * T:(c + 1) * T, :].rearrange("(t p) e -> p t e", p=P)).then_inc(x_in[p], 16)

            def store_v(c, p):
                sp.wait_ge(v_ready, c + 1)
                for j in range(JH):
                    sp.dma_start(vscr[p, :, G4 * j:G4 * (j + 1), :].rearrange("h d t -> d h t"), v_sb[:, j, :]).then_inc(v_stored, 16)

            def load_v(c, p, half):
                if half == 0:
                    sp.wait_ge(v_stored, 16 * JH * (c + 1))
                if c >= 1:
                    sp.wait_ge(kv_ready, NQ * (c - 1) + (NQ - 1 if half == 0 else NQ))
                heads = H // HF
                src = vscr[p].rearrange("h d t -> h (d t)")[half * heads:(half + 1) * heads]
                src = src.unsqueeze(1).broadcast_to([heads, S, S * T])
                sp.dma_start(vrep[:, half].rearrange("p d t -> p (d t)"), src).then_inc(v_in_half[half], 16)

            def load_res(c, p):
                if c >= 1:
                    sp.wait_ge(out_ready, c)
                sp.dma_start(xres[:, :, :], x[c * T:(c + 1) * T, :].rearrange("(t p) e -> p t e", p=P)).then_inc(res_in, 16)

            def store_out(c, p):
                sp.wait_ge(out_ready, c + 1)
                sp.dma_start(out[c * T:(c + 1) * T, :].rearrange("(t p) e -> p t e", p=P), ob[:, :, :]).then_inc(out_stored, 16)

            load_x(0, 0)
            sp.dma_start(vec_sb[:, :], vecs).then_inc(in_small, 16)
            sp.dma_start(const_sb[:, :], consts).then_inc(in_small, 16)
            sp.dma_start(prev_sb[:, :, :, :], prev).then_inc(in_small, 16)
            sp.dma_start(w1_sb[:, :, :], w1).then_inc(in_w, 16)
            sp.dma_start(w2_sb[:, :, :], w2).then_inc(in_w, 16)
            sp.dma_start(dw1_sb[:, :, :], dw1).then_inc(in_w, 16)
            sp.dma_start(dw2_sb[:, :], dw2).then_inc(in_w, 16)
            sp.dma_start(large_sb[:, :, :, :], large).then_inc(in_large, 16)
            sp.dma_start(s0_sb[:, :, :, :], s0).then_inc(in_large, 16)

            def step(i, p):
                if i + 1 < NCH:
                    load_x(i + 1, 1 - p)
                if i < NCH:
                    store_v(i, p)
                if 0 <= i - 2:
                    store_out(i - 2, p)
                if 0 <= i - 1 < NCH:
                    load_res(i - 1, 1 - p)
                if i < NCH:
                    load_v(i, p, 0)
                    load_v(i, p, 1)

            for i in range(NCH + 2):
                step(i, i % 2)
            sp.wait_ge(out_stored, 16 * NCH)
            sp.wait_ge(v_stored, 16 * JH * NCH)



        @block.gpsimd
        def _(pool):
            pool.memset(w_sb[:, :, :, :, 0:1], 0.0).then_inc(inited, 1)
            pool.memset(eps_sb[:, :], EPS).then_inc(inited, 1)
            pool.memset(neg_half[:, :], -0.5).then_inc(inited, 1)
            pool.wait_ge(inited, 3)
            pool.wait_ge(in_small, 48)
            pool.tensor_scalar(gn_half[:, :], vec_sb[:, COL["gn_w"]:COL["gn_w"] + 2 * HF], 0.5, None, ALU.mult).then_inc(halved, 1)

            def put_prev(c, dst, row, done):
                src = prev_sb[:, row, :, c * NB:(c + 1) * NB]
                d = dst[:, :, 0:1].rearrange("p (a b) o -> p a (b o)", a=HF)
                pool.tensor_copy(d, src).then_inc(done, 1)

            def rstd_of(c, mv, rs, added, done, mv_ready):
                pool.wait_ge(mv_ready, c + 1)
                pool.tensor_scalar(rs[:, :], mv[:, :, 1], EPS, None, ALU.add).then_inc(added, 1)
                pool.wait_ge(added, c + 1)
                pool.tensor_tensor(rs[:, :], rs[:, :], neg_half[:, :], ALU.pow).then_inc(done, 1)

            def put_s0(c, q):
                j, half = divmod(q, HF)
                if c > 0 or q >= 2:
                    pool.wait_ge(summed, NQ * c + q - 1)
                pool.tensor_copy(kv[:, q % 2, :, :, 0],
                                 s0_sb[:, half, G4 * j:G4 * (j + 1), c * NB:(c + 1) * NB]).then_inc(s0_put, 1)

            def step(i, p):
                if i < NCH:
                    if i >= 1:
                        pool.wait_ge(x5_ready, 5 * i)
                    put_prev(i, xnp, 1, prev1_put)
                    rstd_of(i, mv1, rs1, eps1_added, rstd1_ready, mv1_ready)
                if 0 <= i - 1 < NCH:
                    if i == 1:
                        pool.wait_ge(in_large, 32)
                    put_s0(i - 1, 0)
                    put_s0(i - 1, 1)
                if 0 <= i - 2:
                    if i - 2 >= 1:
                        pool.wait_ge(xr_ready, i - 2)
                    put_prev(i - 2, xn2p, 0, prev2_put)
                    rstd_of(i - 2, mv2, rs2, eps2_added, rstd2_ready, mv2_ready)
                if 0 <= i - 1 < NCH:
                    put_s0(i - 1, 2)
                    put_s0(i - 1, 3)

            for i in range(NCH + 2):
                step(i, i % 2)

        @block.vector
        def _(dve):
            def layer_norm(c, src, st, mv, rs, dst, st_sem, mv_sem, rs_sem, done):
                for t in range(TT):
                    ins = dve.bn_stats(st[:, t, :], src[:, t, :])
                ins.then_inc(st_sem, 1)
                dve.wait_ge(st_sem, c + 1)
                for t in range(TT):
                    ins = dve.bn_aggr(mv[:, t, :], st[:, t, :])
                ins.then_inc(mv_sem, 1)

            def normalize(c, src, mv, rs, dst, rs_sem, done):
                dve.wait_ge(rs_sem, c + 1)
                for t in range(TT):
                    dve.tensor_scalar(dst[:, t, :], src[:, t, :], mv[:, t, 0:1], rs[:, t:t + 1],
                                      ALU.subtract, ALU.mult).then_inc(done, 1)

            def a_stats(c, p):
                dve.wait_ge(x_in[p], 16 * (c // 2 + 1))
                layer_norm(c, x_tok[:, p], st1, mv1, rs1, xhat, st1_ready, mv1_ready, rstd1_ready, xhat_ready)

            def a_norm(c, p):
                if c >= 1:
                    dve.wait_ge(t1_done, c)
                normalize(c, x_tok[:, p], mv1, rs1, xhat, rstd1_ready, xhat_ready)

            def a_shift(c, p):
                dve.wait_ge(xn_ready, HF * (c + 1))
                dve.wait_ge(prev1_put, c + 1)
                dve.tensor_tensor(sx[:, :, :].rearrange("p a (b t) -> p (a b) t", b=NB),
                                  xnp[:, :, 0:L], xnp[:, :, 1:L + 1], ALU.subtract).then_inc(sx_ready, 1)
                dve.wait_ge(sx_ready, c + 1)
                if c >= 1:
                    dve.wait_ge(w1_done, c)
                for a in range(HF):
                    ins = dve.scalar_tensor_tensor(out=by_seq(mix[:, a]), in0=by_seq(sx[:, a]), scalar=vec("maa_x", a),
                                                   in1=xnp[:, NB * a:NB * (a + 1), 1:L + 1], op0=ALU.mult, op1=ALU.add)
                ins.then_inc(mix_ready, 1)

            def a_mix(c, p, n):
                g = MIXES[n]
                src = pa if n == 0 else pb
                dve.wait_ge(x_done, 5 * c + n + 1)
                if n >= 2:
                    dve.wait_ge([pv_done, pk_done, d1_done][n - 2], c + 1)
                elif c >= 1:
                    dve.wait_ge([pg_done, pg_done][n], c)
                slot = x5_slot(n)
                for a in range(HF):
                    ins = dve.scalar_tensor_tensor(out=x5[:, slot, a], in0=src[:, a], scalar=vec(f"maa{g}", a),
                                                   in1=sx[:, a], op0=ALU.add, op1=ALU.mult)
                ins.then_inc(mixed, 1)
                dve.wait_ge(mixed, 5 * c + n + 1)
                dst = x5[:, slot].rearrange("p a (b t) -> p (a b) t", b=NB)
                dve.tensor_tensor(dst, dst, xnp[:, :, 1:L + 1], ALU.add).then_inc(x5_ready, 1)

            def a_rk(c, p):
                dve.wait_ge(r_ready, c + 1)
                dve.wait_ge(k_ready, c + 1)
                if c >= 2:
                    dve.wait_ge(xr_ready, c - 1)
                for a in range(HF):
                    ins = dve.scalar_tensor_tensor(out=rk[:, a], in0=r_sb[:, p, a], scalar=vec("u", a),
                                                   in1=k_sb[:, p, a], op0=ALU.mult, op1=ALU.mult)
                ins.then_inc(rk_ready, 1)

            def a_bonus(c, p):
                dve.wait_ge(cb_done, c + 1)
                dve.tensor_tensor(bonus[:, p], v_sb[:, :, :], pb[:, 0:1, :].broadcast_to([P, JH, T]), ALU.mult).then_inc(bonus_ready, 1)

            def a_gate(c, p):
                dve.wait_ge(tg_ready, c + 1)
                dve.scalar_tensor_tensor(out=sg[:, p], in0=tg[:, :, :], scalar=1.0, in1=pa[:, :, :],
                                         op0=ALU.add, op1=ALU.mult).then_inc(sg_ready, 1)

            def b_quad(c, p, q):
                j, half = divmod(q, HF)
                if q == 0:
                    dve.wait_ge(k_ready, c + 1)
                    dve.wait_ge(r_ready, c + 1)
                    dve.wait_ge(w_ready, c + 1)
                if q < HF:
                    dve.wait_ge(v_in_half[half], 16 * (c + 1))
                if c > 0 or q >= 2:
                    dve.wait_ge(summed, NQ * c + q - 1)
                buf = kv[:, q % 2]
                kk = by_seq(k_sb[:, p, half])[:, :, 0:L - 1]
                vv = vrep[:, half, G4 * j:G4 * (j + 1), :].rearrange("p d (b t) -> p d b t", b=NB)
                for d in range(G4):
                    ins = dve.tensor_tensor(buf[:, d, :, 1:L], vv[:, d, :, 0:L - 1], kk, ALU.mult)
                ins.then_inc(kv_ready, 1)
                dve.wait_ge(kv_ready, NQ * c + q + 1)
                dve.wait_ge(s0_put, NQ * c + q + 1)
                for d in range(G4):
                    flat = buf[:, d].rearrange("p b t -> p (b t)")
                    ins = dve.tensor_tensor_scan(flat, w_sb[:, p, half].rearrange("p b t -> p (b t)"), flat, 0.0, ALU.mult, ALU.add)
                ins.then_inc(state_ready, 1)
                dve.wait_ge(state_ready, NQ * c + q + 1)
                flat = buf.rearrange("p d b t -> p d (b t)")
                dve.tensor_tensor(flat, flat, r_sb[:, p, half:half + 1, :].broadcast_to([P, G4, T]), ALU.mult).then_inc(rs_ready, 1)

            def c_att(c, p):
                dve.wait_ge(summed, NQ * (c + 1))
                if c >= 1:
                    dve.wait_ge(wo_done, c)
                dve.wait_ge(bonus_ready, c + 1)
                dve.tensor_tensor(att[:, :, :], patt[:, :, :], bonus[:, p], ALU.add).then_inc(att_ready, 1)

            def c_center(c, p):
                dve.wait_ge(mean_done, c + 1)
                dve.tensor_tensor(att[:, :, :], att[:, :, :], pc[:, 0:1, :].broadcast_to([P, JH, T]), ALU.subtract).then_inc(cen_ready, 1)

            def c_gate(c, p):
                dve.wait_ge(rstd_ready, c + 1)
                dve.wait_ge(halved, 1)
                for j in range(JH):
                    ins = dve.scalar_tensor_tensor(out=att[:, j], in0=att[:, j], scalar=gn_half[:, j:j + 1],
                                                   in1=rstd[:, :], op0=ALU.mult, op1=ALU.mult)
                ins.then_inc(scaled, 1)
                dve.wait_ge(scaled, c + 1)
                dve.wait_ge(sg_ready, c + 1)
                for j in range(JH):
                    ins = dve.scalar_tensor_tensor(out=att[:, j], in0=att[:, j], scalar=gn_half[:, HF + j:HF + j + 1],
                                                   in1=sg[:, p, j], op0=ALU.add, op1=ALU.mult)
                ins.then_inc(y_ready, 1)

            def c_res(c, p):
                dve.wait_ge(wo_done, c + 1)
                dve.wait_ge(res_in, 16 * (c + 1))
                dve.tensor_tensor(xres[:, :, :], xres[:, :, :], pc_tok, ALU.add).then_inc(x2_ready, 1)
                dve.wait_ge(x2_ready, c + 1)
                layer_norm(c, xres, st2, mv2, rs2, xhat2, st2_ready, mv2_ready, rstd2_ready, xhat2_ready)

            def c_norm(c, p):
                if c >= 1:
                    dve.wait_ge(out_stored, 16 * c)
                normalize(c, xres, mv2, rs2, xhat2, rstd2_ready, xhat2_ready)

            def c_shift(c, p):
                dve.wait_ge(xn2_ready, HF * (c + 1))
                dve.wait_ge(prev2_put, c + 1)
                dve.tensor_tensor(sx2[:, :, :].rearrange("p a (b t) -> p (a b) t", b=NB),
                                  xn2p[:, :, 0:L], xn2p[:, :, 1:L + 1], ALU.subtract).then_inc(sx2_ready, 1)
                dve.wait_ge(sx2_ready, c + 1)
                for dst, name, done in ((xk, "ffn_k", xk_ready), (xr, "ffn_r", xr_ready)):
                    for a in range(HF):
                        ins = dve.scalar_tensor_tensor(out=by_seq(dst[:, a]), in0=by_seq(sx2[:, a]), scalar=vec(name, a),
                                                       in1=xn2p[:, NB * a:NB * (a + 1), 1:L + 1], op0=ALU.mult, op1=ALU.add)
                    ins.then_inc(done, 1)

            def c_out(c, p):
                dve.wait_ge(y2_done, c + 1)
                dve.wait_ge(trr_ready, c + 1)
                dve.scalar_tensor_tensor(out=trr[:, :, :], in0=trr[:, :, :], scalar=1.0, in1=pc_tok,
                                         op0=ALU.add, op1=ALU.mult).then_inc(gated, 1)
                dve.wait_ge(gated, c + 1)
                dve.scalar_tensor_tensor(out=ob[:, :, :], in0=trr[:, :, :], scalar=0.5, in1=xres[:, :, :],
                                         op0=ALU.mult, op1=ALU.add).then_inc(out_ready, 1)

            dve.wait_ge(in_small, 48)

            def step(i, p):
                A, Bc, C = i < NCH, 0 <= i - 1 < NCH, 0 <= i - 2
                a, b, c = i, i - 1, i - 2
                pb_, pcc = 1 - p, p
                if A: a_stats(a, p)
                if C: c_att(c, pcc)
                if A: a_norm(a, p)
                if C: c_center(c, pcc)
                if Bc: b_quad(b, pb_, 0)
                if A: a_shift(a, p)
                if C: c_gate(c, pcc)
                if A: a_mix(a, p, 0)
                if A: a_mix(a, p, 1)
                if C: c_res(c, pcc)
                if Bc: b_quad(b, pb_, 1)
                if A: a_mix(a, p, 2)
                if C: c_norm(c, pcc)
                if A: a_mix(a, p, 3)
                if Bc: b_quad(b, pb_, 2)
                if C: c_shift(c, pcc)
                if A: a_mix(a, p, 4)
                if A: a_rk(a, p)
                if Bc: b_quad(b, pb_, 3)
                if A: a_gate(a, p)
                if A: a_bonus(a, p)
                if C: c_out(c, pcc)

            for i in range(NCH + 2):
                step(i, i % 2)

        @block.scalar
        def _(act):
            def normed(c, src, dst, w, b, done):
                for a in range(HF):
                    act.activation(dst[:, NB * a:NB * (a + 1), 1:L + 1], by_seq(src[:, a]), ACT.Identity,
                                   bias=vec(b, a), scale=vec(w, a)).then_inc(done, 1)

            def a_xn(c, p):
                act.wait_ge(t1_done, c + 1)
                if c >= 1:
                    act.wait_ge(x5_ready, 5 * c)
                normed(c, pa, xnp, "ln1_w", "ln1_b", xn_ready)

            def a_tanh(c, p):
                act.wait_ge(w1_done, c + 1)
                act.activation(th[:, :, :], pb[:, :, :], ACT.Tanh).then_inc(th_ready, 1)

            def a_v(c, p):
                act.wait_ge(pv_done, c + 1)
                if c >= 1:
                    act.wait_ge(bonus_ready, c)
                    act.wait_ge(v_stored, 16 * JH * c)
                act.activation(v_sb[:, :, :], pa[:, :, :], ACT.Copy).then_inc(v_ready, 1)

            def a_k(c, p):
                act.wait_ge(pk_done, c + 1)
                if c >= 2:
                    act.wait_ge(kv_ready, NQ * (c - 1))
                act.activation(k_sb[:, p], pa[:, :, :], ACT.Copy).then_inc(k_ready, 1)

            def a_thd(c, p):
                act.wait_ge(d1_done, c + 1)
                act.activation(thd[:, :], pa[:, 0, :], ACT.Tanh).then_inc(thd_ready, 1)

            def a_r(c, p):
                act.wait_ge(pr_done, c + 1)
                if c >= 2:
                    act.wait_ge(rs_ready, NQ * (c - 1))
                act.activation(r_sb[:, p], pa[:, :, :], ACT.Copy).then_inc(r_ready, 1)

            def a_w(c, p):
                act.wait_ge(d2_done, c + 1)
                for a in range(HF):
                    ins = act.activation(e_buf[:, a], pb[:, a], ACT.Exp, bias=vec("time_decay", a))
                ins.then_inc(e_ready, 1)
                act.wait_ge(e_ready, c + 1)
                if c >= 2:
                    act.wait_ge(state_ready, NQ * (c - 1))
                if c < 2:
                    act.wait_ge(inited, 3)
                act.activation(w_sb[:, p, :, :, 1:L].rearrange("p a b t -> p (a b) t"),
                               e_buf[:, :, :].rearrange("p a (b t) -> p (a b) t", b=NB)[:, :, 0:L - 1],
                               ACT.Exp, scale=-1.0).then_inc(w_ready, 1)

            def a_tg(c, p):
                act.wait_ge(pg_done, c + 1)
                act.wait_ge(w_ready, c + 1)
                act.activation(tg[:, :, :], pa[:, :, :], ACT.Tanh, scale=0.5).then_inc(tg_ready, 1)

            def c_sq(c, p):
                act.wait_ge(cen_ready, c + 1)
                act.activation(sq[:, :, :], att[:, :, :], ACT.Square).then_inc(sq_ready, 1)

            def c_rstd(c, p):
                act.wait_ge(var_done, c + 1)
                if c >= 1:
                    act.wait_ge(scaled, c)
                act.activation(rstd[:, :], pc[:, 1, :], ACT.Ln, bias=eps_sb[:, 0:1]).then_inc(ln_ready, 1)
                act.wait_ge(ln_ready, c + 1)
                act.activation(rstd[:, :], rstd[:, :], ACT.Exp, scale=-0.5).then_inc(rstd_ready, 1)

            def c_xn(c, p):
                act.wait_ge(t2_done, c + 1)
                if c >= 1:
                    act.wait_ge(xr_ready, c)
                normed(c, pc, xn2p, "ln2_w", "ln2_b", xn2_ready)

            def c_rr(c, p):
                act.wait_ge(rr_done, c + 1)
                if c >= 1:
                    act.wait_ge(out_ready, c)
                act.activation(trr[:, :, :], pc_tok, ACT.Tanh, scale=0.5).then_inc(trr_ready, 1)

            def c_kk(c, p):
                act.wait_ge(kk_done, c + 1)
                if c >= 1:
                    act.wait_ge(y2_done, c)
                act.activation(kk_buf[:, :, :], pc[:, :, :], ACT.Relu).then_inc(relu_ready, 1)
                act.wait_ge(relu_ready, c + 1)
                act.activation(kk_buf[:, :, :], kk_buf[:, :, :], ACT.Square).then_inc(kk_ready, 1)

            act.wait_ge(in_small, 48)
            act.wait_ge(inited, 3)

            def step(i, p):
                A, C = i < NCH, 0 <= i - 2
                a, c = i, i - 2
                if A: a_xn(a, p)
                if C: c_sq(c, p)
                if C: c_rstd(c, p)
                if A: a_tanh(a, p)
                if A: a_v(a, p)
                if A: a_k(a, p)
                if C: c_xn(c, p)
                if A: a_thd(a, p)
                if C: c_rr(c, p)
                if A: a_r(a, p)
                if A: a_w(a, p)
                if C: c_kk(c, p)
                if A: a_tg(a, p)

            for i in range(NCH + 2):
                step(i, i % 2)

        @block.tensor
        def _(pe):
            def transposes(dst, src, done):
                for a in range(HF):
                    for t in range(TT):
                        ins = pe.transpose(dst[:, a, t * P:(t + 1) * P], src[:, t, a * P:(a + 1) * P], ident)
                ins.then_inc(done, 1)

            def project(dst, w, src, done):
                for m in range(HF):
                    for a in range(HF):
                        ins = pe.matmul(dst[:, m], w(a)[:, m * P:(m + 1) * P], src[:, a], start=(a == 0), stop=(a == HF - 1))
                ins.then_inc(done, 1)

            def project_tok(w, src, done):
                for t in range(TT):
                    for a in range(HF):
                        ins = pe.matmul(pc_tok[:, t], src[:, a, t * P:(t + 1) * P], w(a), start=(a == 0), stop=(a == HF - 1))
                ins.then_inc(done, 1)

            def t1(c, p):
                pe.wait_ge(xhat_ready, TT * (c + 1))
                if c >= 1:
                    pe.wait_ge(sg_ready, c)
                transposes(pa, xhat, t1_done)

            def w1_unit(c, p):
                pe.wait_ge(mix_ready, c + 1)
                if c >= 1:
                    pe.wait_ge(bonus_ready, c)
                project(pb, lambda a: w1_sb[:, a, :], mix, w1_done)

            def x_unit(c, p, n):
                g = MIXES[n]
                if n == 0:
                    pe.wait_ge(th_ready, c + 1)
                    pe.wait_ge(xn_ready, HF * (c + 1))
                elif n >= 2:
                    pe.wait_ge(mixed, 5 * c + n)
                dst = pa if n == 0 else pb
                for m in range(HF):
                    ins = pe.matmul(dst[:, m], w2_sb[:, g, m * P:(m + 1) * P], th[:, 0 if g < 4 else 1, :], start=True, stop=True)
                ins.then_inc(x_done, 1)

            def p_unit(c, p, n, name, freed, done):
                pe.wait_ge(x5_ready, 5 * c + n + 1)
                if freed is not None:
                    pe.wait_ge(freed, c + 1)
                project(pa, lambda a: weight(name, a), x5[:, x5_slot(n)], done)

            def d1(c, p):
                pe.wait_ge(x5_ready, 5 * c + 3)
                pe.wait_ge(k_ready, c + 1)
                for a in range(HF):
                    ins = pe.matmul(pa[:, 0], dw1_sb[:, a, :], x5[:, x5_slot(2), a], start=(a == 0), stop=(a == HF - 1))
                ins.then_inc(d1_done, 1)

            def d2(c, p):
                pe.wait_ge(thd_ready, c + 1)
                pe.wait_ge(mixed, 5 * (c + 1))
                for m in range(HF):
                    ins = pe.matmul(pb[:, m], dw2_sb[:, m * P:(m + 1) * P], thd[:, :], start=True, stop=True)
                ins.then_inc(d2_done, 1)

            def cb(c, p):
                pe.wait_ge(rk_ready, c + 1)
                pe.wait_ge(e_ready, c + 1)
                for a in range(HF):
                    ins = pe.matmul(pb[:, 0], sum_k_wide[:, a, :], rk[:, a], start=(a == 0), stop=(a == HF - 1))
                ins.then_inc(cb_done, 1)

            def sums(c, p, q):
                j, half = divmod(q, HF)
                pe.wait_ge(rs_ready, NQ * c + q + 1)
                if q == 0 and c >= 1:
                    pe.wait_ge(att_ready, c)
                for d in range(G4):
                    ins = pe.matmul(patt[d * H:(d + 1) * H, j, :], sum_k[:, half, :],
                                    kv[:, q % 2, d].rearrange("p b t -> p (b t)"), start=(half == 0), stop=(half == HF - 1))
                ins.then_inc(summed, 1)

            def mean(c, p):
                pe.wait_ge(att_ready, c + 1)
                if c >= 1:
                    pe.wait_ge(gated, c)
                for j in range(JH):
                    ins = pe.matmul(pc[:, 0], head_mean, att[:, j], start=(j == 0), stop=(j == JH - 1))
                ins.then_inc(mean_done, 1)

            def var(c, p):
                pe.wait_ge(sq_ready, c + 1)
                for j in range(JH):
                    ins = pe.matmul(pc[:, 1], head_mean, sq[:, j], start=(j == 0), stop=(j == JH - 1))
                ins.then_inc(var_done, 1)

            def wo(c, p):
                pe.wait_ge(y_ready, c + 1)
                project_tok(lambda a: weight("Wo", a), att, wo_done)

            def t2(c, p):
                pe.wait_ge(xhat2_ready, TT * (c + 1))
                transposes(pc, xhat2, t2_done)

            def rr(c, p):
                pe.wait_ge(xr_ready, c + 1)
                project_tok(lambda a: weight("Fr", a), xr, rr_done)

            def kk(c, p):
                pe.wait_ge(trr_ready, c + 1)
                project(pc, lambda a: weight("Fk", a), xk, kk_done)

            def y2(c, p):
                pe.wait_ge(kk_ready, c + 1)
                project_tok(lambda a: weight("Fv", a), kk_buf, y2_done)

            pe.wait_ge(in_small, 48)
            pe.wait_ge(in_w, 64)
            pe.wait_ge(in_large, 32)

            def step(i, p):
                A, Bc, C = i < NCH, 0 <= i - 1 < NCH, 0 <= i - 2
                a, b, c = i, i - 1, i - 2
                if C: mean(c, p)
                if A: t1(a, p)
                if C: var(c, p)
                if Bc: sums(b, 1 - p, 0)
                if A: w1_unit(a, p)
                if A: x_unit(a, p, 0)
                if A: x_unit(a, p, 1)
                if C: wo(c, p)
                if A: p_unit(a, p, 0, "Wv", None, pv_done)
                if A: x_unit(a, p, 2)
                if A: p_unit(a, p, 1, "Wk", v_ready, pk_done)
                if A: x_unit(a, p, 3)
                if Bc: sums(b, 1 - p, 1)
                if C: t2(c, p)
                if A: d1(a, p)
                if A: x_unit(a, p, 4)
                if A: p_unit(a, p, 3, "Wr", thd_ready, pr_done)
                if Bc: sums(b, 1 - p, 2)
                if C: rr(c, p)
                if C: kk(c, p)
                if A: d2(a, p)
                if A: p_unit(a, p, 4, "Wg", r_ready, pg_done)
                if Bc: sums(b, 1 - p, 3)
                if A: cb(a, p)
                if C: y2(c, p)

            for i in range(NCH + 2):
                step(i, i % 2)


def kernel(x, ctx_2048, **w):
    import numpy as np
    import concourse.bacc as bacc
    from concourse.bass_utils import run_bass_kernel_spmd as run

    w = {name[len("L0_xattn_"):]: np.asarray(a) for name, a in w.items()}
    x, state = np.asarray(x), np.asarray(ctx_2048)

    def halves(a):
        return np.ascontiguousarray(a.reshape(HF, P, -1).transpose(1, 0, 2))

    def dh(a):
        return a.reshape(*a.shape[:-1], H, S).swapaxes(-1, -2).reshape(a.shape)

    by_name = {"ln1_w": w["ln1_w"], "ln1_b": w["ln1_b"], "ln2_w": w["ln2_w"], "ln2_b": w["ln2_b"], "maa_x": w["maa_x"],
               **{f"maa{g}": w["maa_stack"][g] for g in range(5)}, "time_decay": w["time_decay"],
               "u": w["faaaa"].reshape(E), "gn_w": dh(w["gn_w"]), "gn_b": dh(w["gn_b"]),
               "ffn_k": w["ffn_maa_k"], "ffn_r": w["ffn_maa_r"]}
    vecs = np.concatenate([by_name[n].reshape(HF, P).T for n in VECS], axis=1)
    w1 = np.zeros((E, 2 * P), np.float32)
    w1[:, 0:5 * LORA] = w["maa_w1"]
    w2 = np.zeros((P, 5, E), np.float32)
    for g in range(5):
        row = LORA * g if g < 4 else 0
        w2[row:row + LORA, g] = w["maa_w2"][g]
    dw1 = np.zeros((E, P), np.float32)
    dw1[:, 0:DECAY] = w["decay_w1"]
    dw2 = np.zeros((P, E), np.float32)
    dw2[0:DECAY] = w["decay_w2"]
    mats = {"Wr": w["Wr"].T, "Wk": w["Wk"].T, "Wv": dh(w["Wv"].T), "Wg": dh(w["Wg"].T), "Wo": dh(w["Wo"]).T,
            "Fk": w["ffn_Wk"].T, "Fr": w["ffn_Wr"].T, "Fv": w["ffn_Wv"].T}
    large = np.stack([halves(mats[n]) for n in LARGE], axis=1)
    prev = np.stack([halves(state[:, row].T) for row in range(2)], axis=1)
    s0 = halves(state[:, 2:2 + S].reshape(B, E, S).transpose(1, 2, 0).reshape(E, S * B))
    rows = np.arange(P)
    head_mean = (rows[:, None] % H == rows[None, :] % H) / np.float32(S)
    wide = np.stack([(rows[:, None] // S + a * (P // S) == rows[None, :] % H) for a in range(HF)], axis=1)
    narrow = wide[:, :, 0:H]
    consts = np.concatenate([np.eye(P), head_mean, wide.reshape(P, -1), narrow.reshape(P, -1)], axis=1).astype(np.float32)

    arrays = {"x": x.reshape(B * L, E), "prev": prev, "s0": s0.reshape(P, HF, S, B), "vecs": vecs, "w1": halves(w1), "w2": w2,
              "dw1": halves(dw1), "dw2": dw2, "large": large, "consts": consts}
    nc = bacc.Bacc("TRN2", target_bir_lowering=False, num_devices=1)
    args = []
    for name in list(arrays):
        a = np.ascontiguousarray(arrays.pop(name))
        arrays["in_" + name] = a
        args.append(nc.dram_tensor("in_" + name, a.shape, F32, kind="ExternalInput").ap())
    args.append(nc.dram_tensor("out", (B * L, E), F32, kind="ExternalOutput").ap())
    build(nc, *args)
    r = run(nc, [arrays], core_ids=[0])
    return r.results[0]["out"].reshape(B, L, E)
```

```python
from contextlib import ExitStack

import concourse.bass as bass
from concourse import mybir

F32 = mybir.dt.float32
ALU = mybir.AluOpType
ACT = mybir.ActivationFunctionType

B, L, E, H = 64, 64, 256, 32
S = E // H
LORA, DECAY = 32, 64
EPS = 1e-5
P = 128
HF = E // P
NB = 8
T = NB * L
NCH = B // NB
TT = T // P
G4 = P // H
JH = S // G4
NQ = JH * HF

DVE_ORDER = [("att", 4), ("sc0", 3), ("a1", 3), ("sg", 3), ("rs0", 3), ("out", 5), ("bonus", 3), ("shift", 2),
             ("cen", 4), ("sc1", 3), ("a2", 3), ("rs1", 3), ("mix0", 2), ("gate", 4), ("mix1", 2), ("sc2", 3),
             ("res", 4), ("st", 0), ("mix2", 2), ("rs2", 3), ("mix3", 2), ("a3", 3), ("shift2", 4),
             ("mix4", 2), ("sc3", 3), ("rk", 2), ("rs3", 3), ("a0", 2)]
PE_ORDER = [("Y2", 5), ("T1", 2), ("S0", 3), ("M", 4), ("W1", 2), ("VR", 4), ("X0", 2), ("X1", 2), ("S1", 3),
            ("P0", 2), ("WO", 4), ("X2", 2), ("P1", 2), ("X3", 2), ("D1", 2), ("T2", 4), ("X4", 2), ("P3", 2),
            ("S2", 3), ("RR", 4), ("D2", 2), ("KK", 4), ("S3", 3), ("P4", 2), ("CB", 2)]
ACT_ORDER = [("nrm", 2), ("xn", 2), ("sq", 4), ("th", 2), ("rstd", 4), ("v", 2), ("k", 2), ("nrm2", 4),
             ("thd", 2), ("xn2", 4), ("r", 2), ("rr", 4), ("w", 2), ("kk", 4), ("tg", 2)]
POOL_ORDER = [("prev2", 4), ("s02", 3), ("s03", 3), ("rd1", 1), ("rd2", 4), ("s00", 2), ("prev1", 1),
              ("s01", 2)]
SP_ORDER = [("lx", 0), ("lr", 4), ("so", 5), ("vst", 2), ("vl0", 2), ("vl1", 2)]
LAGS = 5
VECS = ["ln1_w", "ln1_b", "ln2_w", "ln2_b", "maa_x", "maa0", "maa1", "maa2", "maa3", "maa4",
        "time_decay", "u", "gn_w", "gn_b", "ffn_k", "ffn_r"]
COL = {name: HF * n for n, name in enumerate(VECS)}
MIX_K, MIX_W, MIX_V, MIX_R, MIX_G = range(5)
MIXES = [MIX_V, MIX_K, MIX_W, MIX_R, MIX_G]
LARGE = ["Wr", "Wk", "Wv", "Wg", "Wo", "Fk", "Fr", "Fv"]


def build(nc, x, prev, s0, vecs, w1, w2, dw1, dw2, large, consts, out):
    vscr = nc.dram_tensor("v_scratch", [2, H, S, T], F32, kind="Internal").ap()
    with ExitStack() as ctx:
        def sb(name, shape):
            return ctx.enter_context(nc.sbuf_tensor(name, shape, F32))

        def sem(name):
            return ctx.enter_context(nc.semaphore(name))

        prev_sb = sb("prev_sb", [P, 2, HF, B])
        s0_sb = sb("s0_sb", [P, HF, S, B])
        vec_sb = sb("vec_sb", [P, HF * len(VECS)])
        w1_sb = sb("w1_sb", [P, HF, 2 * P])
        w2_sb = sb("w2_sb", [P, 5, E])
        dw1_sb = sb("dw1_sb", [P, HF, P])
        dw2_sb = sb("dw2_sb", [P, E])
        large_sb = sb("large_sb", [P, len(LARGE), HF, E])
        const_sb = sb("const_sb", [P, 2 * P + HF * P + HF * H])
        gn_half = sb("gn_half", [P, 2 * HF])
        eps_sb = sb("eps_sb", [P, 1])
        neg_half = sb("neg_half", [P, TT])
        ident = const_sb[:, 0:P]
        head_mean = const_sb[:, P:2 * P]
        sum_k_wide = const_sb[:, 2 * P:2 * P + HF * P].rearrange("p (a m) -> p a m", a=HF)
        sum_k = const_sb[:, 2 * P + HF * P:].rearrange("p (a m) -> p a m", a=HF)

        x_tok = sb("x_tok", [P, 2, TT, E])
        st1 = sb("st1", [P, TT, 6])
        mv1 = sb("mv1", [P, TT, 2])
        rs1 = sb("rs1", [P, TT])
        sh1 = sb("sh1", [P, TT])
        xhat = sb("xhat", [P, TT, E])
        xnp = sb("xnp", [P, HF * NB, L + 1])
        sx = sb("sx", [P, HF, T])
        mix = sb("mix", [P, HF, T])
        th = sb("th", [P, 2, T])
        x5 = sb("x5", [P, 3, HF, T])
        v_sb = sb("v_sb", [P, JH, T])
        k_sb = sb("k_sb", [P, 2, HF, T])
        r_sb = sb("r_sb", [P, 2, HF, T])
        w_sb = sb("w_sb", [P, 2, HF, NB, L])
        thd = sb("thd", [P, T])
        sg = sb("sg", [P, 2, JH, T])
        bonus = sb("bonus", [P, 2, JH, T])
        vrep = sb("vrep", [P, HF, S, T])
        kv = sb("kv", [P, 2, G4, NB, L])
        att = sb("att", [P, JH, T])
        sq = sb("sq", [P, JH, T])
        rstd = sb("rstd", [P, T])
        xres = sb("xres", [P, TT, E])
        st2 = sb("st2", [P, TT, 6])
        mv2 = sb("mv2", [P, TT, 2])
        rs2 = sb("rs2", [P, TT])
        sh2 = sb("sh2", [P, TT])
        xn2p = sb("xn2p", [P, HF * NB, L + 1])
        xk = sb("xk", [P, HF, T])
        xr = sb("xr", [P, HF, T])
        trr = sb("trr", [P, TT, E])
        ob = sb("ob", [P, TT, E])

        pa = ctx.enter_context(nc.psum_tensor("pa", [P, 2, T], F32))
        pb = ctx.enter_context(nc.psum_tensor("pb", [P, 2, T], F32))
        pc = ctx.enter_context(nc.psum_tensor("pc", [P, 2, T], F32))
        patt = ctx.enter_context(nc.psum_tensor("patt", [P, JH, T], F32))
        pc_tok = pc[:, :, :].rearrange("p a (t e) -> p (a t) e", e=E)

        in_small, in_w, in_large = sem("in_small"), sem("in_w"), sem("in_large")
        x_in = [sem("x_in0"), sem("x_in1")]
        res_in, v_stored, v_in, out_stored = sem("res_in"), sem("v_stored"), sem("v_in"), sem("out_stored")
        inited, halved, prev1_put, prev2_put, s0_put = [sem(n) for n in ("inited", "halved", "prev1_put", "prev2_put", "s0_put")]
        begun1, powered1, scale1_ready, begun2, powered2, scale2_ready = [sem(n) for n in ("begun1", "powered1", "scale1_ready", "begun2", "powered2", "scale2_ready")]
        st1_ready, mv1_ready, xhat_ready, sx_ready, mix_ready = [sem(n) for n in ("st1_ready", "mv1_ready", "xhat_ready", "sx_ready", "mix_ready")]
        mixed, x5_ready, rk_ready, bonus_ready, sg_ready = [sem(n) for n in ("mixed", "x5_ready", "rk_ready", "bonus_ready", "sg_ready")]
        kv_ready, state_ready, rs_ready = [sem(n) for n in ("kv_ready", "state_ready", "rs_ready")]
        att_ready, cen_ready, scaled, y_ready, x2_ready = [sem(n) for n in ("att_ready", "cen_ready", "scaled", "y_ready", "x2_ready")]
        st2_ready, mv2_ready, xhat2_ready, sx2_ready, xk_ready, xr_ready = [sem(n) for n in ("st2_ready", "mv2_ready", "xhat2_ready", "sx2_ready", "xk_ready", "xr_ready")]
        gated, out_ready = sem("gated"), sem("out_ready")
        xn_ready, th_ready, v_ready, k_ready, thd_ready, r_ready = [sem(n) for n in ("xn_ready", "th_ready", "v_ready", "k_ready", "thd_ready", "r_ready")]
        e_ready, w_ready, tg_ready, sq_ready, ln_ready, rstd_ready = [sem(n) for n in ("e_ready", "w_ready", "tg_ready", "sq_ready", "ln_ready", "rstd_ready")]
        xn2_ready, trr_ready, relu_ready, kk_ready = [sem(n) for n in ("xn2_ready", "trr_ready", "relu_ready", "kk_ready")]
        t1_done, w1_done, x_done, pv_done, pk_done, d1_done, pr_done, d2_done, pg_done, cb_done = [
            sem(n) for n in ("t1_done", "w1_done", "x_done", "pv_done", "pk_done", "d1_done", "pr_done", "d2_done", "pg_done", "cb_done")]
        summed, mean_done, var_done, wo_done, t2_done, rr_done, kk_done, y2_done = [
            sem(n) for n in ("summed", "mean_done", "var_done", "wo_done", "t2_done", "rr_done", "kk_done", "y2_done")]

        tg = sb("tg", [P, JH, T])
        e_buf, rk, kk_buf, xhat2, sx2 = tg, th, sq, ob, sq

        def vec(name, half):
            return vec_sb[:, COL[name] + half:COL[name] + half + 1]

        def weight(name, kt):
            return large_sb[:, LARGE.index(name), kt, :]

        def by_seq(ap):
            return ap.rearrange("p (b t) -> p b t", b=NB)

        v_in_half = [v_in, sem("v_in1")]

        def x5_slot(n):
            return n % 3

        block = ctx.enter_context(nc.Block())

        @block.sync
        def _(sp):
            def load_x(c, p):
                if c >= 2:
                    sp.wait_ge(xhat_ready, TT * (c - 1))
                sp.dma_start(x_tok[:, p], x[c * T:(c + 1) * T, :].rearrange("(t p) e -> p t e", p=P)).then_inc(x_in[p], 16)

            def load_next(c, p):
                if c >= 2:
                    load_x(c, p)

            def store_v(c, p):
                sp.wait_ge(v_ready, c + 1)
                for j in range(JH):
                    sp.dma_start(vscr[p, :, G4 * j:G4 * (j + 1), :].rearrange("h d t -> d h t"), v_sb[:, j, :]).then_inc(v_stored, 16)

            def load_v(c, p, half):
                if half == 0:
                    sp.wait_ge(v_stored, 16 * JH * (c + 1))
                if c >= 1:
                    sp.wait_ge(kv_ready, NQ * (c - 1) + (NQ - 1 if half == 0 else NQ))
                heads = H // HF
                src = vscr[p].rearrange("h d t -> h (d t)")[half * heads:(half + 1) * heads]
                src = src.unsqueeze(1).broadcast_to([heads, S, S * T])
                sp.dma_start(vrep[:, half].rearrange("p d t -> p (d t)"), src).then_inc(v_in_half[half], 16)

            def load_res(c, p):
                if c >= 1:
                    sp.wait_ge(out_ready, c)
                sp.dma_start(xres[:, :, :], x[c * T:(c + 1) * T, :].rearrange("(t p) e -> p t e", p=P)).then_inc(res_in, 16)

            def store_out(c, p):
                sp.wait_ge(out_ready, c + 1)
                sp.dma_start(out[c * T:(c + 1) * T, :].rearrange("(t p) e -> p t e", p=P), ob[:, :, :]).then_inc(out_stored, 16)

            load_x(0, 0)
            load_x(1, 1)
            sp.dma_start(vec_sb[:, :], vecs).then_inc(in_small, 16)
            sp.dma_start(const_sb[:, :], consts).then_inc(in_small, 16)
            sp.dma_start(prev_sb[:, :, :, :], prev).then_inc(in_small, 16)
            sp.dma_start(w1_sb[:, :, :], w1).then_inc(in_w, 16)
            sp.dma_start(w2_sb[:, :, :], w2).then_inc(in_w, 16)
            sp.dma_start(dw1_sb[:, :, :], dw1).then_inc(in_w, 16)
            sp.dma_start(dw2_sb[:, :], dw2).then_inc(in_w, 16)
            sp.dma_start(large_sb[:, :, :, :], large).then_inc(in_large, 16)
            sp.dma_start(s0_sb[:, :, :, :], s0).then_inc(in_large, 16)

            stages = {
                "lx": load_next, "vst": store_v, "vl0": lambda c, p: load_v(c, p, 0), "vl1": lambda c, p: load_v(c, p, 1),
                "lr": load_res, "so": store_out}
            for i in range(NCH + LAGS):
                for name, lag in SP_ORDER:
                    if 0 <= i - lag < NCH:
                        stages[name](i - lag, (i - lag) % 2)
            sp.wait_ge(out_stored, 16 * NCH)
            sp.wait_ge(v_stored, 16 * JH * NCH)



        @block.gpsimd
        def _(pool):
            pool.memset(w_sb[:, :, :, :, 0:1], 0.0).then_inc(inited, 1)
            pool.memset(eps_sb[:, :], EPS).then_inc(inited, 1)
            pool.memset(neg_half[:, :], -0.5).then_inc(inited, 1)
            pool.wait_ge(inited, 3)
            pool.wait_ge(in_small, 48)
            pool.tensor_scalar(gn_half[:, :], vec_sb[:, COL["gn_w"]:COL["gn_w"] + 2 * HF], 0.5, None, ALU.mult).then_inc(halved, 1)

            def put_prev(c, dst, row, done):
                src = prev_sb[:, row, :, c * NB:(c + 1) * NB]
                d = dst[:, :, 0:1].rearrange("p (a b) o -> p a (b o)", a=HF)
                pool.tensor_copy(d, src).then_inc(done, 1)

            def token_scale(c, mv, rs, sh, begun, powered, done, mv_ready, used):
                pool.wait_ge(mv_ready, c + 1)
                if c >= 1:
                    pool.wait_ge(used, TT * c)
                pool.tensor_scalar(rs[:, :], mv[:, :, 1], EPS, None, ALU.add)
                pool.tensor_scalar(sh[:, :], mv[:, :, 0], -1.0, None, ALU.mult).then_inc(begun, 1)
                pool.wait_ge(begun, c + 1)
                pool.tensor_tensor(rs[:, :], rs[:, :], neg_half[:, :], ALU.pow).then_inc(powered, 1)
                pool.wait_ge(powered, c + 1)
                pool.tensor_tensor(sh[:, :], sh[:, :], rs[:, :], ALU.mult).then_inc(done, 1)

            def put_s0(c, q):
                j, half = divmod(q, HF)
                if c > 0 or q >= 2:
                    pool.wait_ge(summed, NQ * c + q - 1)
                pool.tensor_copy(kv[:, q % 2, :, :, 0],
                                 s0_sb[:, half, G4 * j:G4 * (j + 1), c * NB:(c + 1) * NB]).then_inc(s0_put, 1)

            def a_prev(c):
                if c >= 1:
                    pool.wait_ge(x5_ready, 5 * c)
                put_prev(c, xnp, 1, prev1_put)

            def c_prev(c):
                if c >= 1:
                    pool.wait_ge(xr_ready, c)
                put_prev(c, xn2p, 0, prev2_put)

            stages = {
                "prev1": a_prev, "prev2": c_prev,
                "rd1": lambda c: token_scale(c, mv1, rs1, sh1, begun1, powered1, scale1_ready, mv1_ready, xhat_ready),
                "rd2": lambda c: token_scale(c, mv2, rs2, sh2, begun2, powered2, scale2_ready, mv2_ready, xhat2_ready),
                **{f"s0{q}": (lambda c, q=q: put_s0(c, q)) for q in range(NQ)}}
            pool.wait_ge(in_large, 32)
            for i in range(NCH + LAGS):
                for name, lag in POOL_ORDER:
                    if 0 <= i - lag < NCH:
                        stages[name](i - lag)

        @block.vector
        def _(dve):
            def moments(c, src, st, mv, st_sem, mv_sem, used):
                if c >= 1:
                    dve.wait_ge(used, c)
                for t in range(TT):
                    ins = dve.bn_stats(st[:, t, :], src[:, t, :])
                ins.then_inc(st_sem, 1)
                dve.wait_ge(st_sem, c + 1)
                for t in range(TT):
                    ins = dve.bn_aggr(mv[:, t, :], st[:, t, :])
                ins.then_inc(mv_sem, 1)

            def a_stats(c, p):
                dve.wait_ge(x_in[p], 16 * (c // 2 + 1))
                moments(c, x_tok[:, p], st1, mv1, st1_ready, mv1_ready, scale1_ready)

            def a_shift(c, p):
                dve.wait_ge(xn_ready, HF * (c + 1))
                dve.wait_ge(prev1_put, c + 1)
                dve.tensor_tensor(sx[:, :, :].rearrange("p a (b t) -> p (a b) t", b=NB),
                                  xnp[:, :, 0:L], xnp[:, :, 1:L + 1], ALU.subtract).then_inc(sx_ready, 1)
                dve.wait_ge(sx_ready, c + 1)
                if c >= 1:
                    dve.wait_ge(w1_done, c)
                for a in range(HF):
                    ins = dve.scalar_tensor_tensor(out=by_seq(mix[:, a]), in0=by_seq(sx[:, a]), scalar=vec("maa_x", a),
                                                   in1=xnp[:, NB * a:NB * (a + 1), 1:L + 1], op0=ALU.mult, op1=ALU.add)
                ins.then_inc(mix_ready, 1)

            def a_mix(c, p, n):
                g = MIXES[n]
                src = pa if n == 0 else pb
                dve.wait_ge(x_done, 5 * c + n + 1)
                if n >= 3:
                    dve.wait_ge([pv_done, pk_done][n - 3], c + 1)
                elif c >= 1:
                    dve.wait_ge([pr_done, pg_done, d1_done][n], c)
                slot = x5_slot(n)
                for a in range(HF):
                    ins = dve.scalar_tensor_tensor(out=x5[:, slot, a], in0=src[:, a], scalar=vec(f"maa{g}", a),
                                                   in1=sx[:, a], op0=ALU.add, op1=ALU.mult)
                ins.then_inc(mixed, 1)
                dve.wait_ge(mixed, 5 * c + n + 1)
                dst = x5[:, slot].rearrange("p a (b t) -> p (a b) t", b=NB)
                dve.tensor_tensor(dst, dst, xnp[:, :, 1:L + 1], ALU.add).then_inc(x5_ready, 1)

            def a_rk(c, p):
                dve.wait_ge(r_ready, c + 1)
                dve.wait_ge(k_ready, c + 1)
                dve.wait_ge(x_done, 5 * (c + 1))
                for a in range(HF):
                    ins = dve.scalar_tensor_tensor(out=rk[:, a], in0=r_sb[:, p, a], scalar=vec("u", a),
                                                   in1=k_sb[:, p, a], op0=ALU.mult, op1=ALU.mult)
                ins.then_inc(rk_ready, 1)

            def a_bonus(c, p):
                dve.wait_ge(cb_done, c + 1)
                if c >= 2:
                    dve.wait_ge(att_ready, c - 1)
                dve.tensor_tensor(bonus[:, p], v_sb[:, :, :], pb[:, 0:1, :].broadcast_to([P, JH, T]), ALU.mult).then_inc(bonus_ready, 1)

            def a_gate(c, p):
                dve.wait_ge(tg_ready, c + 1)
                if c >= 2:
                    dve.wait_ge(y_ready, c - 1)
                dve.scalar_tensor_tensor(out=sg[:, p], in0=tg[:, :, :], scalar=1.0, in1=pa[:, :, :],
                                         op0=ALU.add, op1=ALU.mult).then_inc(sg_ready, 1)

            def b_products(c, p, q):
                j, half = divmod(q, HF)
                dve.wait_ge(k_ready, c + 1)
                dve.wait_ge(v_in_half[half], 16 * (c + 1))
                if c > 0 or q >= 2:
                    dve.wait_ge(summed, NQ * c + q - 1)
                kk = by_seq(k_sb[:, p, half])[:, :, 0:L - 1]
                vv = vrep[:, half, G4 * j:G4 * (j + 1), :].rearrange("p d (b t) -> p d b t", b=NB)
                for d in range(G4):
                    ins = dve.tensor_tensor(kv[:, q % 2, d, :, 1:L], vv[:, d, :, 0:L - 1], kk, ALU.mult)
                ins.then_inc(kv_ready, 1)

            def b_scan(c, p, q):
                dve.wait_ge(kv_ready, NQ * c + q + 1)
                dve.wait_ge(s0_put, NQ * c + q + 1)
                dve.wait_ge(w_ready, c + 1)
                for d in range(G4):
                    flat = kv[:, q % 2, d].rearrange("p b t -> p (b t)")
                    ins = dve.tensor_tensor_scan(flat, w_sb[:, p, q % HF].rearrange("p b t -> p (b t)"), flat, 0.0, ALU.mult, ALU.add)
                ins.then_inc(state_ready, 1)

            def b_read(c, p, q):
                dve.wait_ge(state_ready, NQ * c + q + 1)
                dve.wait_ge(r_ready, c + 1)
                flat = kv[:, q % 2].rearrange("p d b t -> p d (b t)")
                dve.tensor_tensor(flat, flat, r_sb[:, p, q % HF:q % HF + 1, :].broadcast_to([P, G4, T]), ALU.mult).then_inc(rs_ready, 1)

            def c_att(c, p):
                dve.wait_ge(summed, NQ * (c + 1))
                if c >= 1:
                    dve.wait_ge(wo_done, c)
                dve.wait_ge(bonus_ready, c + 1)
                dve.tensor_tensor(att[:, :, :], patt[:, :, :], bonus[:, p], ALU.add).then_inc(att_ready, 1)

            def c_center(c, p):
                dve.wait_ge(mean_done, c + 1)
                dve.tensor_tensor(att[:, :, :], att[:, :, :], pc[:, 0:1, :].broadcast_to([P, JH, T]), ALU.subtract).then_inc(cen_ready, 1)

            def c_gate(c, p):
                dve.wait_ge(rstd_ready, c + 1)
                dve.wait_ge(halved, 1)
                for j in range(JH):
                    ins = dve.scalar_tensor_tensor(out=att[:, j], in0=att[:, j], scalar=gn_half[:, j:j + 1],
                                                   in1=rstd[:, :], op0=ALU.mult, op1=ALU.mult)
                ins.then_inc(scaled, 1)
                dve.wait_ge(scaled, c + 1)
                dve.wait_ge(sg_ready, c + 1)
                for j in range(JH):
                    ins = dve.scalar_tensor_tensor(out=att[:, j], in0=att[:, j], scalar=gn_half[:, HF + j:HF + j + 1],
                                                   in1=sg[:, p, j], op0=ALU.add, op1=ALU.mult)
                ins.then_inc(y_ready, 1)

            def c_res(c, p):
                dve.wait_ge(wo_done, c + 1)
                dve.wait_ge(res_in, 16 * (c + 1))
                dve.tensor_tensor(xres[:, :, :], xres[:, :, :], pc_tok, ALU.add).then_inc(x2_ready, 1)
                dve.wait_ge(x2_ready, c + 1)
                moments(c, xres, st2, mv2, st2_ready, mv2_ready, scale2_ready)

            def c_shift(c, p):
                dve.wait_ge(xn2_ready, HF * (c + 1))
                dve.wait_ge(prev2_put, c + 1)
                dve.tensor_tensor(sx2[:, :, :].rearrange("p a (b t) -> p (a b) t", b=NB),
                                  xn2p[:, :, 0:L], xn2p[:, :, 1:L + 1], ALU.subtract).then_inc(sx2_ready, 1)
                dve.wait_ge(sx2_ready, c + 1)
                for dst, name, done in ((xk, "ffn_k", xk_ready), (xr, "ffn_r", xr_ready)):
                    for a in range(HF):
                        ins = dve.scalar_tensor_tensor(out=by_seq(dst[:, a]), in0=by_seq(sx2[:, a]), scalar=vec(name, a),
                                                       in1=xn2p[:, NB * a:NB * (a + 1), 1:L + 1], op0=ALU.mult, op1=ALU.add)
                    ins.then_inc(done, 1)

            def c_out(c, p):
                dve.wait_ge(y2_done, c + 1)
                dve.wait_ge(trr_ready, c + 1)
                dve.scalar_tensor_tensor(out=trr[:, :, :], in0=trr[:, :, :], scalar=1.0, in1=pc_tok,
                                         op0=ALU.add, op1=ALU.mult).then_inc(gated, 1)
                dve.wait_ge(gated, c + 1)
                dve.scalar_tensor_tensor(out=ob[:, :, :], in0=trr[:, :, :], scalar=0.5, in1=xres[:, :, :],
                                         op0=ALU.mult, op1=ALU.add).then_inc(out_ready, 1)

            dve.wait_ge(in_small, 48)

            stages = {
                "st": a_stats, "shift": a_shift, "rk": a_rk, "bonus": a_bonus, "sg": a_gate,
                **{f"mix{n}": (lambda c, p, n=n: a_mix(c, p, n)) for n in range(5)},
                **{f"a{q}": (lambda c, p, q=q: b_products(c, p, q)) for q in range(NQ)},
                **{f"sc{q}": (lambda c, p, q=q: b_scan(c, p, q)) for q in range(NQ)},
                **{f"rs{q}": (lambda c, p, q=q: b_read(c, p, q)) for q in range(NQ)},
                "att": c_att, "cen": c_center, "gate": c_gate, "res": c_res, "shift2": c_shift, "out": c_out}
            for i in range(NCH + LAGS):
                for name, lag in DVE_ORDER:
                    if 0 <= i - lag < NCH:
                        stages[name](i - lag, (i - lag) % 2)

        @block.scalar
        def _(act):
            def normed(c, src, dst, w, b, done):
                for a in range(HF):
                    act.activation(dst[:, NB * a:NB * (a + 1), 1:L + 1], by_seq(src[:, a]), ACT.Identity,
                                   bias=vec(b, a), scale=vec(w, a)).then_inc(done, 1)

            def normalize(c, src, rs, sh, dst, scale_ready, done):
                act.wait_ge(scale_ready, c + 1)
                for t in range(TT):
                    act.activation(dst[:, t, :], src[:, t, :], ACT.Identity, scale=rs[:, t:t + 1],
                                   bias=sh[:, t:t + 1]).then_inc(done, 1)

            def a_norm(c, p):
                if c >= 1:
                    act.wait_ge(t1_done, c)
                normalize(c, x_tok[:, p], rs1, sh1, xhat, scale1_ready, xhat_ready)

            def c_norm(c, p):
                if c >= 1:
                    act.wait_ge(out_stored, 16 * c)
                normalize(c, xres, rs2, sh2, xhat2, scale2_ready, xhat2_ready)

            def a_xn(c, p):
                act.wait_ge(t1_done, c + 1)
                if c >= 1:
                    act.wait_ge(x5_ready, 5 * c)
                normed(c, pa, xnp, "ln1_w", "ln1_b", xn_ready)

            def a_tanh(c, p):
                act.wait_ge(w1_done, c + 1)
                if c >= 1:
                    act.wait_ge(cb_done, c)
                act.activation(th[:, :, :], pb[:, :, :], ACT.Tanh).then_inc(th_ready, 1)

            def a_v(c, p):
                act.wait_ge(pv_done, c + 1)
                if c >= 1:
                    act.wait_ge(bonus_ready, c)
                    act.wait_ge(v_stored, 16 * JH * c)
                act.activation(v_sb[:, :, :], pa[:, :, :], ACT.Copy).then_inc(v_ready, 1)

            def a_k(c, p):
                act.wait_ge(pk_done, c + 1)
                if c >= 2:
                    act.wait_ge(kv_ready, NQ * (c - 1))
                act.activation(k_sb[:, p], pa[:, :, :], ACT.Copy).then_inc(k_ready, 1)

            def a_thd(c, p):
                act.wait_ge(d1_done, c + 1)
                act.activation(thd[:, :], pa[:, 0, :], ACT.Tanh).then_inc(thd_ready, 1)

            def a_r(c, p):
                act.wait_ge(pr_done, c + 1)
                if c >= 2:
                    act.wait_ge(rs_ready, NQ * (c - 1))
                act.activation(r_sb[:, p], pa[:, :, :], ACT.Copy).then_inc(r_ready, 1)

            def a_w(c, p):
                act.wait_ge(d2_done, c + 1)
                if c >= 1:
                    act.wait_ge(sg_ready, c)
                for a in range(HF):
                    ins = act.activation(e_buf[:, a], pb[:, a], ACT.Exp, bias=vec("time_decay", a))
                ins.then_inc(e_ready, 1)
                act.wait_ge(e_ready, c + 1)
                if c >= 2:
                    act.wait_ge(state_ready, NQ * (c - 1))
                if c < 2:
                    act.wait_ge(inited, 3)
                act.activation(w_sb[:, p, :, :, 1:L].rearrange("p a b t -> p (a b) t"),
                               e_buf[:, :, :].rearrange("p a (b t) -> p (a b) t", b=NB)[:, :, 0:L - 1],
                               ACT.Exp, scale=-1.0).then_inc(w_ready, 1)

            def a_tg(c, p):
                act.wait_ge(pg_done, c + 1)
                act.wait_ge(w_ready, c + 1)
                act.activation(tg[:, :, :], pa[:, :, :], ACT.Tanh, scale=0.5).then_inc(tg_ready, 1)

            def c_sq(c, p):
                act.wait_ge(cen_ready, c + 1)
                act.activation(sq[:, :, :], att[:, :, :], ACT.Square).then_inc(sq_ready, 1)

            def c_rstd(c, p):
                act.wait_ge(var_done, c + 1)
                if c >= 1:
                    act.wait_ge(scaled, c)
                act.activation(rstd[:, :], pc[:, 1, :], ACT.Ln, bias=eps_sb[:, 0:1]).then_inc(ln_ready, 1)
                act.wait_ge(ln_ready, c + 1)
                act.activation(rstd[:, :], rstd[:, :], ACT.Exp, scale=-0.5).then_inc(rstd_ready, 1)

            def c_xn(c, p):
                act.wait_ge(t2_done, c + 1)
                if c >= 1:
                    act.wait_ge(xr_ready, c)
                normed(c, pc, xn2p, "ln2_w", "ln2_b", xn2_ready)

            def c_rr(c, p):
                act.wait_ge(rr_done, c + 1)
                if c >= 1:
                    act.wait_ge(out_ready, c)
                act.activation(trr[:, :, :], pc_tok, ACT.Tanh, scale=0.5).then_inc(trr_ready, 1)

            def c_kk(c, p):
                act.wait_ge(kk_done, c + 1)
                if c >= 1:
                    act.wait_ge(y2_done, c)
                act.activation(kk_buf[:, :, :], pc[:, :, :], ACT.Relu).then_inc(relu_ready, 1)
                act.wait_ge(relu_ready, c + 1)
                act.activation(kk_buf[:, :, :], kk_buf[:, :, :], ACT.Square).then_inc(kk_ready, 1)

            act.wait_ge(in_small, 48)
            act.wait_ge(inited, 3)

            stages = {
                "nrm": a_norm, "xn": a_xn, "th": a_tanh, "v": a_v, "k": a_k, "thd": a_thd, "r": a_r, "w": a_w, "tg": a_tg,
                "sq": c_sq, "rstd": c_rstd, "nrm2": c_norm, "xn2": c_xn, "rr": c_rr, "kk": c_kk}
            for i in range(NCH + LAGS):
                for name, lag in ACT_ORDER:
                    if 0 <= i - lag < NCH:
                        stages[name](i - lag, (i - lag) % 2)

        @block.tensor
        def _(pe):
            def transposes(dst, src, done):
                for a in range(HF):
                    for t in range(TT):
                        ins = pe.transpose(dst[:, a, t * P:(t + 1) * P], src[:, t, a * P:(a + 1) * P], ident)
                ins.then_inc(done, 1)

            def project(dst, w, src, done):
                for m in range(HF):
                    for a in range(HF):
                        ins = pe.matmul(dst[:, m], w(a)[:, m * P:(m + 1) * P], src[:, a], start=(a == 0), stop=(a == HF - 1))
                ins.then_inc(done, 1)

            def project_tok(w, src, done):
                for t in range(TT):
                    for a in range(HF):
                        ins = pe.matmul(pc_tok[:, t], src[:, a, t * P:(t + 1) * P], w(a), start=(a == 0), stop=(a == HF - 1))
                ins.then_inc(done, 1)

            def t1(c, p):
                pe.wait_ge(xhat_ready, TT * (c + 1))
                if c >= 1:
                    pe.wait_ge(sg_ready, c)
                transposes(pa, xhat, t1_done)

            def w1_unit(c, p):
                pe.wait_ge(mix_ready, c + 1)
                if c >= 1:
                    pe.wait_ge(bonus_ready, c)
                project(pb, lambda a: w1_sb[:, a, :], mix, w1_done)

            def x_unit(c, p, n):
                g = MIXES[n]
                if n == 0:
                    pe.wait_ge(th_ready, c + 1)
                    pe.wait_ge(xn_ready, HF * (c + 1))
                elif n >= 2:
                    pe.wait_ge(mixed, 5 * c + n)
                dst = pa if n == 0 else pb
                for m in range(HF):
                    ins = pe.matmul(dst[:, m], w2_sb[:, g, m * P:(m + 1) * P], th[:, 0 if g < 4 else 1, :], start=True, stop=True)
                ins.then_inc(x_done, 1)

            def p_unit(c, p, n, name, freed, done):
                pe.wait_ge(x5_ready, 5 * c + n + 1)
                if c == 0 and n == 0:
                    pe.wait_ge(in_large, 32)
                if freed is not None:
                    pe.wait_ge(freed, c + 1)
                project(pa, lambda a: weight(name, a), x5[:, x5_slot(n)], done)

            def d1(c, p):
                pe.wait_ge(x5_ready, 5 * c + 3)
                pe.wait_ge(k_ready, c + 1)
                for a in range(HF):
                    ins = pe.matmul(pa[:, 0], dw1_sb[:, a, :], x5[:, x5_slot(2), a], start=(a == 0), stop=(a == HF - 1))
                ins.then_inc(d1_done, 1)

            def d2(c, p):
                pe.wait_ge(thd_ready, c + 1)
                pe.wait_ge(mixed, 5 * (c + 1))
                for m in range(HF):
                    ins = pe.matmul(pb[:, m], dw2_sb[:, m * P:(m + 1) * P], thd[:, :], start=True, stop=True)
                ins.then_inc(d2_done, 1)

            def cb(c, p):
                pe.wait_ge(rk_ready, c + 1)
                pe.wait_ge(e_ready, c + 1)
                for a in range(HF):
                    ins = pe.matmul(pb[:, 0], sum_k_wide[:, a, :], rk[:, a], start=(a == 0), stop=(a == HF - 1))
                ins.then_inc(cb_done, 1)

            def sums(c, p, q):
                j, half = divmod(q, HF)
                pe.wait_ge(rs_ready, NQ * c + q + 1)
                if q == 0 and c >= 1:
                    pe.wait_ge(att_ready, c)
                for d in range(G4):
                    ins = pe.matmul(patt[d * H:(d + 1) * H, j, :], sum_k[:, half, :],
                                    kv[:, q % 2, d].rearrange("p b t -> p (b t)"), start=(half == 0), stop=(half == HF - 1))
                ins.then_inc(summed, 1)

            def mean(c, p):
                pe.wait_ge(att_ready, c + 1)
                if c >= 1:
                    pe.wait_ge(gated, c)
                for j in range(JH):
                    ins = pe.matmul(pc[:, 0], head_mean, att[:, j], start=(j == 0), stop=(j == JH - 1))
                ins.then_inc(mean_done, 1)

            def var(c, p):
                pe.wait_ge(sq_ready, c + 1)
                for j in range(JH):
                    ins = pe.matmul(pc[:, 1], head_mean, sq[:, j], start=(j == 0), stop=(j == JH - 1))
                ins.then_inc(var_done, 1)

            def wo(c, p):
                pe.wait_ge(y_ready, c + 1)
                project_tok(lambda a: weight("Wo", a), att, wo_done)

            def t2(c, p):
                pe.wait_ge(xhat2_ready, TT * (c + 1))
                transposes(pc, xhat2, t2_done)

            def rr(c, p):
                pe.wait_ge(xr_ready, c + 1)
                project_tok(lambda a: weight("Fr", a), xr, rr_done)

            def kk(c, p):
                pe.wait_ge(trr_ready, c + 1)
                project(pc, lambda a: weight("Fk", a), xk, kk_done)

            def y2(c, p):
                pe.wait_ge(kk_ready, c + 1)
                project_tok(lambda a: weight("Fv", a), kk_buf, y2_done)

            pe.wait_ge(in_small, 48)
            pe.wait_ge(in_w, 64)

            stages = {
                "T1": t1, "W1": w1_unit, **{f"X{n}": (lambda c, p, n=n: x_unit(c, p, n)) for n in range(5)},
                "P0": lambda c, p: p_unit(c, p, 0, "Wv", None, pv_done),
                "P1": lambda c, p: p_unit(c, p, 1, "Wk", v_ready, pk_done),
                "D1": d1, "D2": d2, "CB": cb,
                "P3": lambda c, p: p_unit(c, p, 3, "Wr", thd_ready, pr_done),
                "P4": lambda c, p: p_unit(c, p, 4, "Wg", r_ready, pg_done),
                **{f"S{q}": (lambda c, p, q=q: sums(c, p, q)) for q in range(NQ)},
                "M": mean, "VR": var, "WO": wo, "T2": t2, "RR": rr, "KK": kk, "Y2": y2}
            for i in range(NCH + LAGS):
                for name, lag in PE_ORDER:
                    if 0 <= i - lag < NCH:
                        stages[name](i - lag, (i - lag) % 2)


def kernel(x, ctx_2048, **w):
    import numpy as np
    import concourse.bacc as bacc
    from concourse.bass_utils import run_bass_kernel_spmd as run

    w = {name[len("L0_xattn_"):]: np.asarray(a) for name, a in w.items()}
    x, state = np.asarray(x), np.asarray(ctx_2048)

    def halves(a):
        return np.ascontiguousarray(a.reshape(HF, P, -1).transpose(1, 0, 2))

    def dh(a):
        return a.reshape(*a.shape[:-1], H, S).swapaxes(-1, -2).reshape(a.shape)

    by_name = {"ln1_w": w["ln1_w"], "ln1_b": w["ln1_b"], "ln2_w": w["ln2_w"], "ln2_b": w["ln2_b"], "maa_x": w["maa_x"],
               **{f"maa{g}": w["maa_stack"][g] for g in range(5)}, "time_decay": w["time_decay"],
               "u": w["faaaa"].reshape(E), "gn_w": dh(w["gn_w"]), "gn_b": dh(w["gn_b"]),
               "ffn_k": w["ffn_maa_k"], "ffn_r": w["ffn_maa_r"]}
    vecs = np.concatenate([by_name[n].reshape(HF, P).T for n in VECS], axis=1)
    w1 = np.zeros((E, 2 * P), np.float32)
    w1[:, 0:5 * LORA] = w["maa_w1"]
    w2 = np.zeros((P, 5, E), np.float32)
    for g in range(5):
        row = LORA * g if g < 4 else 0
        w2[row:row + LORA, g] = w["maa_w2"][g]
    dw1 = np.zeros((E, P), np.float32)
    dw1[:, 0:DECAY] = w["decay_w1"]
    dw2 = np.zeros((P, E), np.float32)
    dw2[0:DECAY] = w["decay_w2"]
    mats = {"Wr": w["Wr"].T, "Wk": w["Wk"].T, "Wv": dh(w["Wv"].T), "Wg": dh(w["Wg"].T), "Wo": dh(w["Wo"]).T,
            "Fk": w["ffn_Wk"].T, "Fr": w["ffn_Wr"].T, "Fv": w["ffn_Wv"].T}
    large = np.stack([halves(mats[n]) for n in LARGE], axis=1)
    prev = np.stack([halves(state[:, row].T) for row in range(2)], axis=1)
    s0 = halves(state[:, 2:2 + S].reshape(B, E, S).transpose(1, 2, 0).reshape(E, S * B))
    rows = np.arange(P)
    head_mean = (rows[:, None] % H == rows[None, :] % H) / np.float32(S)
    wide = np.stack([(rows[:, None] // S + a * (P // S) == rows[None, :] % H) for a in range(HF)], axis=1)
    narrow = wide[:, :, 0:H]
    consts = np.concatenate([np.eye(P), head_mean, wide.reshape(P, -1), narrow.reshape(P, -1)], axis=1).astype(np.float32)

    arrays = {"x": x.reshape(B * L, E), "prev": prev, "s0": s0.reshape(P, HF, S, B), "vecs": vecs, "w1": halves(w1), "w2": w2,
              "dw1": halves(dw1), "dw2": dw2, "large": large, "consts": consts}
    nc = bacc.Bacc("TRN2", target_bir_lowering=False, num_devices=1)
    args = []
    for name in list(arrays):
        a = np.ascontiguousarray(arrays.pop(name))
        arrays["in_" + name] = a
        args.append(nc.dram_tensor("in_" + name, a.shape, F32, kind="ExternalInput").ap())
    args.append(nc.dram_tensor("out", (B * L, E), F32, kind="ExternalOutput").ap())
    build(nc, *args)
    r = run(nc, [arrays], core_ids=[0])
    return r.results[0]["out"].reshape(B, L, E)
```

```python
from contextlib import ExitStack

import concourse.bass as bass
from concourse import mybir

F32 = mybir.dt.float32
ALU = mybir.AluOpType
ACT = mybir.ActivationFunctionType

B, L, E, H = 64, 64, 256, 32
S = E // H
LORA, DECAY = 32, 64
EPS = 1e-5
P = 128
FOLD, DFOLD = P // LORA, P // DECAY
HF = E // P
SEQS = [4, 6, 8, 8, 8, 8, 8, 8, 6]
FIRST = [sum(SEQS[:c]) for c in range(len(SEQS))]
NCH = len(SEQS)
NB = 8
T = NB * L
TT = T // P
assert sum(SEQS) == B and all(2 <= n <= NB and n * L % P == 0 for n in SEQS)
G4 = P // H
JH = S // G4
NQ = JH * HF

DVE_ORDER = [("rk", 2), ("out", 4), ("sc0", 2), ("cen", 3), ("bonus", 2), ("rs0", 2), ("shift", 1), ("a1", 2),
             ("gate", 3), ("sc1", 2), ("mix0", 1), ("res", 3), ("mix1", 1), ("a2", 2), ("mix2", 1), ("rs1", 2),
             ("sc2", 2), ("mix3", 1), ("rs2", 2), ("shift2", 3), ("a3", 2), ("mix4", 1), ("sc3", 2),
             ("rs3", 2), ("a0", 1), ("att", 2)]
PE_ORDER = [("M", 3), ("CB", 2), ("T1", 1), ("VR", 3), ("S0", 2), ("W1", 1), ("X0", 1), ("WO", 3), ("X1", 1),
            ("P0", 1), ("X2", 1), ("P1", 1), ("X3", 1), ("S1", 2), ("D1", 1), ("T2", 3), ("X4", 1), ("P3", 1),
            ("RR", 3), ("S2", 2), ("KK", 3), ("D2", 1), ("S3", 2), ("Y2", 3), ("P4", 1)]
ACT_ORDER = [("w", 2), ("tg", 2), ("sq", 3), ("xn", 1), ("rstd", 3), ("th", 1), ("st", 0), ("v", 1),
             ("st2", 3), ("k", 1), ("nrm2", 3), ("xn2", 3), ("thd", 1), ("nrm", 0), ("rr", 3), ("kk", 3),
             ("r", 1)]
POOL_ORDER = [("prev1", 1), ("s01", 2), ("rd1", 0), ("s02", 2), ("rd2", 3), ("s03", 2), ("s00", 1),
              ("prev2", 2)]
SP_ORDER = [("lx", 0), ("so", 4), ("lr", 3), ("vst", 1), ("vl0", 1), ("vl1", 1)]
LAGS = 4
VECS = ["ln1_w", "ln1_b", "ln2_w", "ln2_b", "maa_x", "maa0", "maa1", "maa2", "maa3", "maa4",
        "time_decay", "u", "gn_w", "gn_b", "ffn_k", "ffn_r"]
COL = {name: HF * n for n, name in enumerate(VECS)}
MIX_K, MIX_W, MIX_V, MIX_R, MIX_G = range(5)
MIXES = [MIX_V, MIX_K, MIX_W, MIX_R, MIX_G]
LARGE = ["Wv", "Wk", "Wr", "Wg", "Wo", "Fr", "Fk", "Fv"]


def extent(c):
    return SEQS[c], SEQS[c] * L, SEQS[c] * L // P


def build(nc, x, prev, s0, vecs, w1, w2, dw1, dw2, large, consts, out):
    vscr = nc.dram_tensor("v_scratch", [2, E * T], F32, kind="Internal").ap()
    with ExitStack() as ctx:
        def sb(name, shape):
            return ctx.enter_context(nc.sbuf_tensor(name, shape, F32))

        def sem(name):
            return ctx.enter_context(nc.semaphore(name))

        prev_sb = sb("prev_sb", [P, 2, HF, B])
        s0_sb = sb("s0_sb", [P, HF, S, B])
        vec_sb = sb("vec_sb", [P, HF * len(VECS)])
        w1_sb = sb("w1_sb", [P, HF, 5 * LORA])
        w2_sb = sb("w2_sb", [P, 4 + FOLD, E])
        dw1_sb = sb("dw1_sb", [P, HF, DECAY])
        dw2_sb = sb("dw2_sb", [P, DFOLD, E])
        large_sb = sb("large_sb", [P, len(LARGE), HF, E])
        const_sb = sb("const_sb", [P, 2 * P + HF * P + HF * H])
        eps_sb = sb("eps_sb", [P, 1])
        neg_half = sb("neg_half", [P, TT])
        ident = const_sb[:, 0:P]
        head_mean = const_sb[:, P:2 * P]
        sum_k_wide = const_sb[:, 2 * P:2 * P + HF * P].rearrange("p (a m) -> p a m", a=HF)
        sum_k = const_sb[:, 2 * P + HF * P:].rearrange("p (a m) -> p a m", a=HF)

        x_tok = sb("x_tok", [P, 2, TT, E])
        mean1 = sb("mean1", [P, TT])
        var1 = sb("var1", [P, TT])
        rs1 = sb("rs1", [P, TT])
        sh1 = sb("sh1", [P, TT])
        xhat = sb("xhat", [P, TT, E])
        xnp = sb("xnp", [P, HF, NB, L + 1])
        sx = sb("sx", [P, HF, T])
        mix = sb("mix", [P, HF, T])
        th = sb("th", [P, 2, T])
        x5 = sb("x5", [P, 3, HF, T])
        v_sb = sb("v_sb", [P, JH, T])
        k_sb = sb("k_sb", [P, 2, HF, T])
        r_sb = sb("r_sb", [P, 2, HF, T])
        w_sb = sb("w_sb", [P, 2, HF, NB, L])
        thd = sb("thd", [P, T // DFOLD])
        sg = sb("sg", [P, 2, JH, T])
        bonus = sb("bonus", [P, 2, JH, T])
        vrep = sb("vrep", [P, HF, S * T])
        kv = sb("kv", [P, 2, G4, NB, L])
        att = sb("att", [P, JH, T])
        sq = sb("sq", [P, JH, T])
        rstd = sb("rstd", [P, T])
        xres = sb("xres", [P, TT, E])
        mean2 = sb("mean2", [P, TT])
        var2 = sb("var2", [P, TT])
        rs2 = sb("rs2", [P, TT])
        sh2 = sb("sh2", [P, TT])
        xn2p = sb("xn2p", [P, HF, NB, L + 1])
        xk = sb("xk", [P, HF, T])
        xr = sb("xr", [P, HF, T])
        trr = sb("trr", [P, TT, E])
        ob = sb("ob", [P, TT, E])

        pa = ctx.enter_context(nc.psum_tensor("pa", [P, 2, T], F32))
        pb = ctx.enter_context(nc.psum_tensor("pb", [P, 2, T], F32))
        pc = ctx.enter_context(nc.psum_tensor("pc", [P, 2, T], F32))
        patt = ctx.enter_context(nc.psum_tensor("patt", [P, JH, T], F32))
        pc_tok = pc[:, :, :].rearrange("p a (t e) -> p (a t) e", e=E)

        in_const, in_vec, in_prev, in_w1, in_w2, in_dw, in_s0 = [
            sem(n) for n in ("in_const", "in_vec", "in_prev", "in_w1", "in_w2", "in_dw", "in_s0")]
        in_vk, in_rg, in_late = [sem(n) for n in ("in_vk", "in_rg", "in_late")]
        LARGE_PARTS = [(["Wv", "Wk"], in_vk), (["Wr", "Wg"], in_rg), (["Wo", "Fv"], in_late)]
        x_in = [sem("x_in0"), sem("x_in1")]
        res_in, v_stored, v_in, out_stored = sem("res_in"), sem("v_stored"), sem("v_in"), sem("out_stored")
        inited, prev1_put, prev2_put, s0_put = [sem(n) for n in ("inited", "prev1_put", "prev2_put", "s0_put")]
        begun1, powered1, scale1_ready, begun2, powered2, scale2_ready = [sem(n) for n in ("begun1", "powered1", "scale1_ready", "begun2", "powered2", "scale2_ready")]
        mean1_ready, var1_ready, xhat_ready, sx_ready, mix_ready = [sem(n) for n in ("mean1_ready", "var1_ready", "xhat_ready", "sx_ready", "mix_ready")]
        mixed, x5_ready, rk_ready, bonus_ready, sg_ready = [sem(n) for n in ("mixed", "x5_ready", "rk_ready", "bonus_ready", "sg_ready")]
        kv_ready, state_ready, rs_ready = [sem(n) for n in ("kv_ready", "state_ready", "rs_ready")]
        att_ready, cen_ready, scaled, y_ready, x2_ready = [sem(n) for n in ("att_ready", "cen_ready", "scaled", "y_ready", "x2_ready")]
        mean2_ready, var2_ready, xhat2_ready, sx2_ready, xk_ready, xr_ready = [sem(n) for n in ("mean2_ready", "var2_ready", "xhat2_ready", "sx2_ready", "xk_ready", "xr_ready")]
        gated, out_ready = sem("gated"), sem("out_ready")
        xn_ready, th_ready, v_ready, k_ready, thd_ready, r_ready = [sem(n) for n in ("xn_ready", "th_ready", "v_ready", "k_ready", "thd_ready", "r_ready")]
        e_ready, w_ready, sq_ready, ln_ready, rstd_ready = [sem(n) for n in ("e_ready", "w_ready", "sq_ready", "ln_ready", "rstd_ready")]
        xn2_ready, trr_ready, relu_ready, kk_ready = [sem(n) for n in ("xn2_ready", "trr_ready", "relu_ready", "kk_ready")]
        t1_done, w1_done, x_done, pv_done, pk_done, d1_done, pr_done, d2_done, pg_done, cb_done = [
            sem(n) for n in ("t1_done", "w1_done", "x_done", "pv_done", "pk_done", "d1_done", "pr_done", "d2_done", "pg_done", "cb_done")]
        summed, mean_done, var_done, wo_done, t2_done, rr_done, kk_done, y2_done = [
            sem(n) for n in ("summed", "mean_done", "var_done", "wo_done", "t2_done", "rr_done", "kk_done", "y2_done")]

        e_buf = sb("e_buf", [P, HF, T])
        rk, kk_buf, xhat2, sx2 = th, sq, ob, sq

        def vec(name, half):
            return vec_sb[:, COL[name] + half:COL[name] + half + 1]

        def weight(name, kt):
            return large_sb[:, LARGE.index(name), kt, :]

        def by_seq(ap):
            return ap.rearrange("p (b t) -> p b t", t=L)

        v_in_half = [v_in, sem("v_in1")]

        def x5_slot(n):
            return n % 3

        def summed_mixes(c, n):
            return 4 * c + (n + 1 if n < 2 else n)

        block = ctx.enter_context(nc.Block())

        @block.sync
        def _(sp):
            def tokens(dram, c):
                n = extent(c)[1]
                return dram[FIRST[c] * L:FIRST[c] * L + n, :].rearrange("(t p) e -> p t e", p=P)

            def scratch(c, p):
                n = extent(c)[1]
                return vscr[p, 0:E * n].rearrange("(h d t) -> h d t", h=H, d=S)

            def load_x(c, p):
                if c >= 2:
                    sp.wait_ge(xhat_ready, c - 1)
                sp.dma_start(x_tok[:, p, 0:extent(c)[2]], tokens(x, c)).then_inc(x_in[p], 16)

            def load_large(names, done):
                lo, hi = LARGE.index(names[0]), LARGE.index(names[-1]) + 1
                sp.dma_start(large_sb[:, lo:hi, :, :], large[:, lo:hi]).then_inc(done, 16)

            def load_next(c, p):
                if c >= 2:
                    load_x(c, p)

            def store_v(c, p):
                sp.wait_ge(v_ready, c + 1)
                for j in range(JH):
                    sp.dma_start(scratch(c, p)[:, G4 * j:G4 * (j + 1), :].rearrange("h d t -> d h t"),
                                 v_sb[:, j, 0:extent(c)[1]]).then_inc(v_stored, 16)

            def load_v(c, p, half):
                if half == 0:
                    sp.wait_ge(v_stored, 16 * JH * (c + 1))
                if c >= 1:
                    sp.wait_ge(kv_ready, NQ * (c - 1) + (NQ - 1 if half == 0 else NQ))
                heads = H // HF
                n = extent(c)[1]
                src = scratch(c, p).rearrange("h d t -> h (d t)")[half * heads:(half + 1) * heads]
                src = src.unsqueeze(1).broadcast_to([heads, S, S * n])
                sp.dma_start(vrep[:, half, 0:S * n], src).then_inc(v_in_half[half], 16)

            def load_res(c, p):
                if c >= 1:
                    sp.wait_ge(out_ready, c)
                sp.dma_start(xres[:, 0:extent(c)[2], :], tokens(x, c)).then_inc(res_in, 16)

            def store_out(c, p):
                sp.wait_ge(out_ready, c + 1)
                sp.dma_start(tokens(out, c), ob[:, 0:extent(c)[2], :]).then_inc(out_stored, 16)

            load_x(0, 0)
            sp.dma_start(const_sb[:, :], consts).then_inc(in_const, 16)
            sp.dma_start(vec_sb[:, :], vecs).then_inc(in_vec, 16)
            sp.dma_start(prev_sb[:, :, :, :], prev).then_inc(in_prev, 16)
            sp.dma_start(w1_sb[:, :, :], w1).then_inc(in_w1, 16)
            sp.dma_start(w2_sb[:, :, :], w2).then_inc(in_w2, 16)
            for names, done in LARGE_PARTS[0:2]:
                load_large(names, done)
            sp.dma_start(dw1_sb[:, :, :], dw1).then_inc(in_dw, 16)
            sp.dma_start(dw2_sb[:, :, :], dw2).then_inc(in_dw, 16)
            load_x(1, 1)
            sp.dma_start(s0_sb[:, :, :, :], s0).then_inc(in_s0, 16)
            for names, done in LARGE_PARTS[2:]:
                load_large(names, done)

            stages = {
                "lx": load_next, "vst": store_v, "vl0": lambda c, p: load_v(c, p, 0), "vl1": lambda c, p: load_v(c, p, 1),
                "lr": load_res, "so": store_out}
            for i in range(NCH + LAGS):
                for name, lag in SP_ORDER:
                    if 0 <= i - lag < NCH:
                        stages[name](i - lag, (i - lag) % 2)
            sp.wait_ge(out_stored, 16 * NCH)
            sp.wait_ge(v_stored, 16 * JH * NCH)



        @block.gpsimd
        def _(pool):
            pool.memset(w_sb[:, :, :, :, 0:1], 0.0).then_inc(inited, 1)
            pool.memset(eps_sb[:, :], EPS).then_inc(inited, 1)
            pool.memset(neg_half[:, :], -0.5).then_inc(inited, 1)
            pool.wait_ge(inited, 3)

            def put_prev(c, dst, row, done):
                if c == 0:
                    pool.wait_ge(in_prev, 16)
                nb = extent(c)[0]
                pool.tensor_copy(dst[:, :, 0:nb, 0], prev_sb[:, row, :, FIRST[c]:FIRST[c] + nb]).then_inc(done, 1)

            def token_scale(c, mean, var, rs, sh, begun, powered, done, var_ready, used):
                pool.wait_ge(var_ready, c + 1)
                if c >= 1:
                    pool.wait_ge(used, c)
                n = extent(c)[2]
                rs, sh = rs[:, 0:n], sh[:, 0:n]
                pool.tensor_scalar(rs, var[:, 0:n], 1.0 / E, EPS, ALU.mult, ALU.add).then_inc(begun, 1)
                pool.wait_ge(begun, c + 1)
                pool.tensor_tensor(rs, rs, neg_half[:, 0:n], ALU.pow).then_inc(powered, 1)
                pool.wait_ge(powered, c + 1)
                pool.tensor_tensor(sh, mean[:, 0:n], rs, ALU.mult).then_inc(done, 1)

            def put_s0(c, q):
                j, half = divmod(q, HF)
                if c > 0 or q >= 2:
                    pool.wait_ge(summed, NQ * c + q - 1)
                if c == 0 and q == 0:
                    pool.wait_ge(in_s0, 16)
                nb = extent(c)[0]
                pool.tensor_copy(kv[:, q % 2, :, 0:nb, 0],
                                 s0_sb[:, half, G4 * j:G4 * (j + 1), FIRST[c]:FIRST[c] + nb]).then_inc(s0_put, 1)

            def a_prev(c):
                if c >= 1:
                    pool.wait_ge(x5_ready, 4 * c)
                    pool.wait_ge(d1_done, c)
                put_prev(c, xnp, 1, prev1_put)

            def c_prev(c):
                if c >= 1:
                    pool.wait_ge(xk_ready, c)
                put_prev(c, xn2p, 0, prev2_put)

            stages = {
                "prev1": a_prev, "prev2": c_prev,
                "rd1": lambda c: token_scale(c, mean1, var1, rs1, sh1, begun1, powered1, scale1_ready, var1_ready, xhat_ready),
                "rd2": lambda c: token_scale(c, mean2, var2, rs2, sh2, begun2, powered2, scale2_ready, var2_ready, xhat2_ready),
                **{f"s0{q}": (lambda c, q=q: put_s0(c, q)) for q in range(NQ)}}
            for i in range(NCH + LAGS):
                for name, lag in POOL_ORDER:
                    if 0 <= i - lag < NCH:
                        stages[name](i - lag)

        @block.vector
        def _(dve):
            def a_shift(c, p):
                dve.wait_ge(xn_ready, c + 1)
                nb, n = extent(c)[0:2]
                dve.wait_ge(prev1_put, c + 1)
                dve.tensor_tensor(sx[:, :, 0:n].rearrange("p a (b t) -> p a b t", t=L),
                                  xnp[:, :, 0:nb, 0:L], xnp[:, :, 0:nb, 1:L + 1], ALU.subtract).then_inc(sx_ready, 1)
                dve.wait_ge(sx_ready, c + 1)
                if c >= 1:
                    dve.wait_ge(w1_done, c)
                for a in range(HF):
                    ins = dve.scalar_tensor_tensor(out=by_seq(mix[:, a, 0:n]), in0=by_seq(sx[:, a, 0:n]), scalar=vec("maa_x", a),
                                                   in1=xnp[:, a, 0:nb, 1:L + 1], op0=ALU.mult, op1=ALU.add)
                ins.then_inc(mix_ready, 1)

            def a_mix(c, p, n):
                g = MIXES[n]
                nb, nt = extent(c)[0:2]
                src = pa if n == 0 else pb
                dve.wait_ge(x_done, 5 * c + n + 1)
                if n >= 3:
                    dve.wait_ge([pv_done, pk_done][n - 3], c + 1)
                elif c >= 1:
                    dve.wait_ge([pr_done, pg_done, d1_done][n], c)
                slot = x5_slot(n)
                for a in range(HF):
                    ins = dve.scalar_tensor_tensor(out=x5[:, slot, a, 0:nt], in0=src[:, a, 0:nt], scalar=vec(f"maa{g}", a),
                                                   in1=sx[:, a, 0:nt], op0=ALU.add, op1=ALU.mult)
                ins.then_inc(mixed, 1)
                if g == MIX_W:
                    return
                dve.wait_ge(mixed, 5 * c + n + 1)
                dst = x5[:, slot, :, 0:nt].rearrange("p a (b t) -> p a b t", t=L)
                dve.tensor_tensor(dst, dst, xnp[:, :, 0:nb, 1:L + 1], ALU.add).then_inc(x5_ready, 1)

            def a_rk(c, p):
                dve.wait_ge(r_ready, c + 1)
                dve.wait_ge(k_ready, c + 1)
                dve.wait_ge(x_done, 5 * (c + 1))
                n = extent(c)[1]
                for a in range(HF):
                    ins = dve.scalar_tensor_tensor(out=rk[:, a, 0:n], in0=r_sb[:, p, a, 0:n], scalar=vec("u", a),
                                                   in1=k_sb[:, p, a, 0:n], op0=ALU.mult, op1=ALU.mult)
                ins.then_inc(rk_ready, 1)

            def a_bonus(c, p):
                dve.wait_ge(cb_done, c + 1)
                if c >= 2:
                    dve.wait_ge(att_ready, c - 1)
                n = extent(c)[1]
                dve.tensor_tensor(bonus[:, p, :, 0:n], v_sb[:, :, 0:n], pb[:, 0:1, 0:n].broadcast_to([P, JH, n]), ALU.mult).then_inc(bonus_ready, 1)

            def b_products(c, p, q):
                j, half = divmod(q, HF)
                dve.wait_ge(k_ready, c + 1)
                dve.wait_ge(v_in_half[half], 16 * (c + 1))
                if c > 0 or q >= 2:
                    dve.wait_ge(summed, NQ * c + q - 1)
                nb, n = extent(c)[0:2]
                kk = by_seq(k_sb[:, p, half, 0:n])[:, :, 0:L - 1]
                vv = vrep[:, half, 0:S * n].rearrange("p (d b t) -> p d b t", d=S, t=L)
                for d in range(G4):
                    ins = dve.tensor_tensor(kv[:, q % 2, d, 0:nb, 1:L], vv[:, G4 * j + d, :, 0:L - 1], kk, ALU.mult)
                ins.then_inc(kv_ready, 1)

            def b_scan(c, p, q):
                dve.wait_ge(kv_ready, NQ * c + q + 1)
                dve.wait_ge(s0_put, NQ * c + q + 1)
                dve.wait_ge(w_ready, c + 1)
                nb = extent(c)[0]
                for d in range(G4):
                    flat = kv[:, q % 2, d, 0:nb].rearrange("p b t -> p (b t)")
                    ins = dve.tensor_tensor_scan(flat, w_sb[:, p, q % HF, 0:nb].rearrange("p b t -> p (b t)"), flat, 0.0, ALU.mult, ALU.add)
                ins.then_inc(state_ready, 1)

            def b_read(c, p, q):
                dve.wait_ge(state_ready, NQ * c + q + 1)
                dve.wait_ge(r_ready, c + 1)
                nb, n = extent(c)[0:2]
                flat = kv[:, q % 2, :, 0:nb].rearrange("p d b t -> p d (b t)")
                dve.tensor_tensor(flat, flat, r_sb[:, p, q % HF:q % HF + 1, 0:n].broadcast_to([P, G4, n]), ALU.mult).then_inc(rs_ready, 1)

            def c_att(c, p):
                dve.wait_ge(summed, NQ * (c + 1))
                if c >= 1:
                    dve.wait_ge(wo_done, c)
                dve.wait_ge(bonus_ready, c + 1)
                n = extent(c)[1]
                dve.tensor_tensor(att[:, :, 0:n], patt[:, :, 0:n], bonus[:, p, :, 0:n], ALU.add).then_inc(att_ready, 1)

            def c_center(c, p):
                dve.wait_ge(mean_done, c + 1)
                n = extent(c)[1]
                dve.tensor_tensor(att[:, :, 0:n], att[:, :, 0:n], pc[:, 0:1, 0:n].broadcast_to([P, JH, n]), ALU.subtract).then_inc(cen_ready, 1)

            def c_gate(c, p):
                dve.wait_ge(rstd_ready, c + 1)
                n = extent(c)[1]
                for j in range(JH):
                    ins = dve.scalar_tensor_tensor(out=att[:, j, 0:n], in0=att[:, j, 0:n], scalar=vec("gn_w", j),
                                                   in1=rstd[:, 0:n], op0=ALU.mult, op1=ALU.mult)
                ins.then_inc(scaled, 1)
                dve.wait_ge(scaled, c + 1)
                dve.wait_ge(sg_ready, c + 1)
                for j in range(JH):
                    ins = dve.scalar_tensor_tensor(out=att[:, j, 0:n], in0=att[:, j, 0:n], scalar=vec("gn_b", j),
                                                   in1=sg[:, p, j, 0:n], op0=ALU.add, op1=ALU.mult)
                ins.then_inc(y_ready, 1)

            def c_res(c, p):
                dve.wait_ge(wo_done, c + 1)
                dve.wait_ge(res_in, 16 * (c + 1))
                n = extent(c)[2]
                dve.tensor_tensor(xres[:, 0:n, :], xres[:, 0:n, :], pc_tok[:, 0:n], ALU.add).then_inc(x2_ready, 1)

            def c_shift(c, p):
                dve.wait_ge(xn2_ready, c + 1)
                nb, n = extent(c)[0:2]
                dve.wait_ge(prev2_put, c + 1)
                dve.tensor_tensor(sx2[:, :, 0:n].rearrange("p a (b t) -> p a b t", t=L),
                                  xn2p[:, :, 0:nb, 0:L], xn2p[:, :, 0:nb, 1:L + 1], ALU.subtract).then_inc(sx2_ready, 1)
                dve.wait_ge(sx2_ready, c + 1)
                for dst, name, done in ((xr, "ffn_r", xr_ready), (xk, "ffn_k", xk_ready)):
                    for a in range(HF):
                        ins = dve.scalar_tensor_tensor(out=by_seq(dst[:, a, 0:n]), in0=by_seq(sx2[:, a, 0:n]), scalar=vec(name, a),
                                                       in1=xn2p[:, a, 0:nb, 1:L + 1], op0=ALU.mult, op1=ALU.add)
                    ins.then_inc(done, 1)

            def c_out(c, p):
                dve.wait_ge(y2_done, c + 1)
                dve.wait_ge(trr_ready, c + 1)
                n = extent(c)[2]
                dve.scalar_tensor_tensor(out=trr[:, 0:n, :], in0=trr[:, 0:n, :], scalar=1.0, in1=pc_tok[:, 0:n],
                                         op0=ALU.add, op1=ALU.mult).then_inc(gated, 1)
                dve.wait_ge(gated, c + 1)
                dve.scalar_tensor_tensor(out=ob[:, 0:n, :], in0=trr[:, 0:n, :], scalar=0.5, in1=xres[:, 0:n, :],
                                         op0=ALU.mult, op1=ALU.add).then_inc(out_ready, 1)

            dve.wait_ge(in_vec, 16)

            stages = {
                "shift": a_shift, "rk": a_rk, "bonus": a_bonus,
                **{f"mix{n}": (lambda c, p, n=n: a_mix(c, p, n)) for n in range(5)},
                **{f"a{q}": (lambda c, p, q=q: b_products(c, p, q)) for q in range(NQ)},
                **{f"sc{q}": (lambda c, p, q=q: b_scan(c, p, q)) for q in range(NQ)},
                **{f"rs{q}": (lambda c, p, q=q: b_read(c, p, q)) for q in range(NQ)},
                "att": c_att, "cen": c_center, "gate": c_gate, "res": c_res, "shift2": c_shift, "out": c_out}
            for i in range(NCH + LAGS):
                for name, lag in DVE_ORDER:
                    if 0 <= i - lag < NCH:
                        stages[name](i - lag, (i - lag) % 2)

        @block.scalar
        def _(act):
            def normed(c, src, dst, w, b, done):
                nb, n = extent(c)[0:2]
                for a in range(HF):
                    ins = act.activation(dst[:, a, 0:nb, 1:L + 1], by_seq(src[:, a, 0:n]), ACT.Identity,
                                         bias=vec(b, a), scale=vec(w, a))
                ins.then_inc(done, 1)

            def moments(c, src, mean, var, scratch, mean_ready, var_ready, used):
                if c >= 1:
                    act.wait_ge(used, c)
                for t in range(extent(c)[2]):
                    ins = act.activation(scratch[:, t, :], src[:, t, :], ACT.Copy, scale=-1.0 / E, accum_out=mean[:, t:t + 1])
                ins.then_inc(mean_ready, 1)
                act.wait_ge(mean_ready, c + 1)
                for t in range(extent(c)[2]):
                    ins = act.activation(scratch[:, t, :], src[:, t, :], ACT.Square, bias=mean[:, t:t + 1], accum_out=var[:, t:t + 1])
                ins.then_inc(var_ready, 1)

            def a_moments(c, p):
                act.wait_ge(x_in[p], 16 * (c // 2 + 1))
                if c >= 1:
                    act.wait_ge(t1_done, c)
                moments(c, x_tok[:, p], mean1, var1, xhat, mean1_ready, var1_ready, scale1_ready)

            def c_moments(c, p):
                act.wait_ge(x2_ready, c + 1)
                if c >= 1:
                    act.wait_ge(out_stored, 16 * c)
                moments(c, xres, mean2, var2, xhat2, mean2_ready, var2_ready, scale2_ready)

            def normalize(c, src, rs, sh, dst, scale_ready, done):
                act.wait_ge(scale_ready, c + 1)
                for t in range(extent(c)[2]):
                    ins = act.activation(dst[:, t, :], src[:, t, :], ACT.Identity, scale=rs[:, t:t + 1],
                                         bias=sh[:, t:t + 1])
                ins.then_inc(done, 1)

            def a_norm(c, p):
                normalize(c, x_tok[:, p], rs1, sh1, xhat, scale1_ready, xhat_ready)

            def c_norm(c, p):
                normalize(c, xres, rs2, sh2, xhat2, scale2_ready, xhat2_ready)

            def a_xn(c, p):
                act.wait_ge(t1_done, c + 1)
                if c >= 1:
                    act.wait_ge(x5_ready, 4 * c)
                    act.wait_ge(d1_done, c)
                normed(c, pa, xnp, "ln1_w", "ln1_b", xn_ready)

            def a_tanh(c, p):
                act.wait_ge(w1_done, c + 1)
                if c >= 1:
                    act.wait_ge(cb_done, c)
                n = extent(c)[1]
                act.activation(th[:, 0, 0:n], pb[:, 0, 0:n], ACT.Tanh)
                act.activation(th[:, 1, 0:n // FOLD], pb[:, 1, 0:n // FOLD], ACT.Tanh).then_inc(th_ready, 1)

            def a_v(c, p):
                act.wait_ge(pv_done, c + 1)
                if c >= 1:
                    act.wait_ge(bonus_ready, c)
                    act.wait_ge(v_stored, 16 * JH * c)
                n = extent(c)[1]
                act.activation(v_sb[:, :, 0:n], pa[:, :, 0:n], ACT.Copy).then_inc(v_ready, 1)

            def a_k(c, p):
                act.wait_ge(pk_done, c + 1)
                if c >= 2:
                    act.wait_ge(kv_ready, NQ * (c - 1))
                n = extent(c)[1]
                act.activation(k_sb[:, p, :, 0:n], pa[:, :, 0:n], ACT.Copy).then_inc(k_ready, 1)

            def a_thd(c, p):
                act.wait_ge(d1_done, c + 1)
                nf = extent(c)[1] // DFOLD
                act.activation(thd[:, 0:nf], pa[:, 0, 0:nf], ACT.Tanh).then_inc(thd_ready, 1)

            def a_r(c, p):
                act.wait_ge(pr_done, c + 1)
                if c >= 2:
                    act.wait_ge(rs_ready, NQ * (c - 1))
                n = extent(c)[1]
                act.activation(r_sb[:, p, :, 0:n], pa[:, :, 0:n], ACT.Copy).then_inc(r_ready, 1)

            def a_w(c, p):
                act.wait_ge(d2_done, c + 1)
                if c >= 1:
                    act.wait_ge(w_ready, c)
                nb, n = extent(c)[0:2]
                for a in range(HF):
                    ins = act.activation(e_buf[:, a, 0:n], pb[:, a, 0:n], ACT.Exp, bias=vec("time_decay", a))
                ins.then_inc(e_ready, 1)
                act.wait_ge(e_ready, c + 1)
                if c >= 2:
                    act.wait_ge(state_ready, NQ * (c - 1))
                if c < 2:
                    act.wait_ge(inited, 3)
                act.activation(w_sb[:, p, :, 0:nb, 1:L],
                               e_buf[:, :, 0:n].rearrange("p a (b t) -> p a b t", t=L)[:, :, :, 0:L - 1],
                               ACT.Exp, scale=-1.0).then_inc(w_ready, 1)

            def a_gate(c, p):
                act.wait_ge(pg_done, c + 1)
                if c >= 2:
                    act.wait_ge(y_ready, c - 1)
                n = extent(c)[1]
                act.activation(sg[:, p, :, 0:n], pa[:, :, 0:n], ACT.Silu).then_inc(sg_ready, 1)

            def c_sq(c, p):
                act.wait_ge(cen_ready, c + 1)
                n = extent(c)[1]
                act.activation(sq[:, :, 0:n], att[:, :, 0:n], ACT.Square).then_inc(sq_ready, 1)

            def c_rstd(c, p):
                act.wait_ge(var_done, c + 1)
                if c >= 1:
                    act.wait_ge(scaled, c)
                n = extent(c)[1]
                act.activation(rstd[:, 0:n], pc[:, 1, 0:n], ACT.Ln, bias=eps_sb[:, 0:1]).then_inc(ln_ready, 1)
                act.wait_ge(ln_ready, c + 1)
                act.activation(rstd[:, 0:n], rstd[:, 0:n], ACT.Exp, scale=-0.5).then_inc(rstd_ready, 1)

            def c_xn(c, p):
                act.wait_ge(t2_done, c + 1)
                if c >= 1:
                    act.wait_ge(xk_ready, c)
                normed(c, pc, xn2p, "ln2_w", "ln2_b", xn2_ready)

            def c_rr(c, p):
                act.wait_ge(rr_done, c + 1)
                if c >= 1:
                    act.wait_ge(out_ready, c)
                n = extent(c)[2]
                act.activation(trr[:, 0:n, :], pc_tok[:, 0:n], ACT.Tanh, scale=0.5).then_inc(trr_ready, 1)

            def c_kk(c, p):
                act.wait_ge(kk_done, c + 1)
                if c >= 1:
                    act.wait_ge(y2_done, c)
                n = extent(c)[1]
                act.activation(kk_buf[:, :, 0:n], pc[:, :, 0:n], ACT.Relu).then_inc(relu_ready, 1)
                act.wait_ge(relu_ready, c + 1)
                act.activation(kk_buf[:, :, 0:n], kk_buf[:, :, 0:n], ACT.Square).then_inc(kk_ready, 1)

            act.wait_ge(in_vec, 16)
            act.wait_ge(inited, 3)

            stages = {
                "st": a_moments, "st2": c_moments, "nrm": a_norm, "xn": a_xn, "th": a_tanh, "v": a_v, "k": a_k, "thd": a_thd, "r": a_r, "w": a_w, "tg": a_gate,
                "sq": c_sq, "rstd": c_rstd, "nrm2": c_norm, "xn2": c_xn, "rr": c_rr, "kk": c_kk}
            for i in range(NCH + LAGS):
                for name, lag in ACT_ORDER:
                    if 0 <= i - lag < NCH:
                        stages[name](i - lag, (i - lag) % 2)

        @block.tensor
        def _(pe):
            def transposes(c, dst, src, done):
                for a in range(HF):
                    for t in range(extent(c)[2]):
                        ins = pe.transpose(dst[:, a, t * P:(t + 1) * P], src[:, t, a * P:(a + 1) * P], ident)
                ins.then_inc(done, 1)

            def project(c, dst, w, src, done):
                n = extent(c)[1]
                for m in range(HF):
                    for a in range(HF):
                        ins = pe.matmul(dst[:, m, 0:n], w(a)[:, m * P:(m + 1) * P], src[:, a, 0:n], start=(a == 0), stop=(a == HF - 1))
                ins.then_inc(done, 1)

            def project_tok(c, w, src, done):
                for t in range(extent(c)[2]):
                    for a in range(HF):
                        ins = pe.matmul(pc_tok[:, t], src[:, a, t * P:(t + 1) * P], w(a), start=(a == 0), stop=(a == HF - 1))
                ins.then_inc(done, 1)

            def t1(c, p):
                pe.wait_ge(xhat_ready, c + 1)
                if c >= 1:
                    pe.wait_ge(sg_ready, c)
                transposes(c, pa, xhat, t1_done)

            def w1_unit(c, p):
                if c == 0:
                    pe.wait_ge(in_w1, 16)
                pe.wait_ge(mix_ready, c + 1)
                if c >= 1:
                    pe.wait_ge(bonus_ready, c)
                n = extent(c)[1]
                for a in range(HF):
                    pe.matmul(pb[:, 0, 0:n], w1_sb[:, a, 0:P], mix[:, a, 0:n], start=(a == 0), stop=(a == HF - 1))
                nf = n // FOLD
                for a in range(HF):
                    for f in range(FOLD):
                        ins = pe.matmul(pb[f * LORA:(f + 1) * LORA, 1, 0:nf], w1_sb[:, a, P:P + LORA],
                                        mix[:, a, f * nf:(f + 1) * nf], start=(a == 0), stop=(a == HF - 1))
                ins.then_inc(w1_done, 1)

            def x_unit(c, p, n):
                g = MIXES[n]
                if n == 0:
                    pe.wait_ge(th_ready, c + 1)
                    pe.wait_ge(xn_ready, c + 1)
                    if c == 0:
                        pe.wait_ge(in_w2, 16)
                elif n >= 2:
                    pe.wait_ge(mixed, 5 * c + n)
                dst = pa if n == 0 else pb
                nt = extent(c)[1]
                nf = nt // FOLD
                for m in range(HF):
                    if g < 4:
                        ins = pe.matmul(dst[:, m, 0:nt], w2_sb[:, g, m * P:(m + 1) * P], th[:, 0, 0:nt], start=True, stop=True)
                        continue
                    for f in range(FOLD):
                        ins = pe.matmul(dst[:, m, f * nf:(f + 1) * nf], w2_sb[:, g + f, m * P:(m + 1) * P], th[:, 1, 0:nf],
                                        start=True, stop=True)
                ins.then_inc(x_done, 1)

            def p_unit(c, p, n, name, freed, done):
                pe.wait_ge(x5_ready, summed_mixes(c, n))
                if c == 0 and n in (0, 3):
                    pe.wait_ge(in_vk if n == 0 else in_rg, 16)
                if freed is not None:
                    pe.wait_ge(freed, c + 1)
                project(c, pa, lambda a: weight(name, a), x5[:, x5_slot(n)], done)

            def d1(c, p):
                pe.wait_ge(mixed, 5 * c + 3)
                pe.wait_ge(k_ready, c + 1)
                if c == 0:
                    pe.wait_ge(in_dw, 32)
                n = extent(c)[1]
                nf, bf = n // DFOLD, extent(c)[0] // DFOLD
                for a in range(HF):
                    for f in range(DFOLD):
                        pe.matmul(pa[f * DECAY:(f + 1) * DECAY, 0, 0:nf], dw1_sb[:, a, :],
                                  xnp[:, a, f * bf:(f + 1) * bf, 1:L + 1], start=(a == 0), stop=False)
                for a in range(HF):
                    for f in range(DFOLD):
                        ins = pe.matmul(pa[f * DECAY:(f + 1) * DECAY, 0, 0:nf], dw1_sb[:, a, :],
                                        x5[:, x5_slot(2), a, f * nf:(f + 1) * nf], start=False, stop=(a == HF - 1))
                ins.then_inc(d1_done, 1)

            def d2(c, p):
                pe.wait_ge(thd_ready, c + 1)
                pe.wait_ge(mixed, 5 * (c + 1))
                n = extent(c)[1]
                nf = n // DFOLD
                for m in range(HF):
                    for f in range(DFOLD):
                        ins = pe.matmul(pb[:, m, f * nf:(f + 1) * nf], dw2_sb[:, f, m * P:(m + 1) * P], thd[:, 0:nf],
                                        start=True, stop=True)
                ins.then_inc(d2_done, 1)

            def cb(c, p):
                pe.wait_ge(rk_ready, c + 1)
                pe.wait_ge(e_ready, c + 1)
                n = extent(c)[1]
                for a in range(HF):
                    ins = pe.matmul(pb[:, 0, 0:n], sum_k_wide[:, a, :], rk[:, a, 0:n], start=(a == 0), stop=(a == HF - 1))
                ins.then_inc(cb_done, 1)

            def sums(c, p, q):
                j, half = divmod(q, HF)
                pe.wait_ge(rs_ready, NQ * c + q + 1)
                if q == 0 and c >= 1:
                    pe.wait_ge(att_ready, c)
                nb, n = extent(c)[0:2]
                for d in range(G4):
                    ins = pe.matmul(patt[d * H:(d + 1) * H, j, 0:n], sum_k[:, half, :],
                                    kv[:, q % 2, d, 0:nb].rearrange("p b t -> p (b t)"), start=(half == 0), stop=(half == HF - 1))
                ins.then_inc(summed, 1)

            def mean(c, p):
                pe.wait_ge(att_ready, c + 1)
                if c >= 1:
                    pe.wait_ge(gated, c)
                n = extent(c)[1]
                for j in range(JH):
                    ins = pe.matmul(pc[:, 0, 0:n], head_mean, att[:, j, 0:n], start=(j == 0), stop=(j == JH - 1))
                ins.then_inc(mean_done, 1)

            def var(c, p):
                pe.wait_ge(sq_ready, c + 1)
                n = extent(c)[1]
                for j in range(JH):
                    ins = pe.matmul(pc[:, 1, 0:n], head_mean, sq[:, j, 0:n], start=(j == 0), stop=(j == JH - 1))
                ins.then_inc(var_done, 1)

            def wo(c, p):
                if c == 0:
                    pe.wait_ge(in_late, 16)
                pe.wait_ge(y_ready, c + 1)
                project_tok(c, lambda a: weight("Wo", a), att, wo_done)

            def t2(c, p):
                pe.wait_ge(xhat2_ready, c + 1)
                transposes(c, pc, xhat2, t2_done)

            def rr(c, p):
                pe.wait_ge(xr_ready, c + 1)
                project_tok(c, lambda a: weight("Fr", a), xr, rr_done)

            def kk(c, p):
                pe.wait_ge(xk_ready, c + 1)
                pe.wait_ge(trr_ready, c + 1)
                project(c, pc, lambda a: weight("Fk", a), xk, kk_done)

            def y2(c, p):
                pe.wait_ge(kk_ready, c + 1)
                project_tok(c, lambda a: weight("Fv", a), kk_buf, y2_done)

            pe.wait_ge(in_const, 16)

            stages = {
                "T1": t1, "W1": w1_unit, **{f"X{n}": (lambda c, p, n=n: x_unit(c, p, n)) for n in range(5)},
                "P0": lambda c, p: p_unit(c, p, 0, "Wv", None, pv_done),
                "P1": lambda c, p: p_unit(c, p, 1, "Wk", v_ready, pk_done),
                "D1": d1, "D2": d2, "CB": cb,
                "P3": lambda c, p: p_unit(c, p, 3, "Wr", thd_ready, pr_done),
                "P4": lambda c, p: p_unit(c, p, 4, "Wg", r_ready, pg_done),
                **{f"S{q}": (lambda c, p, q=q: sums(c, p, q)) for q in range(NQ)},
                "M": mean, "VR": var, "WO": wo, "T2": t2, "RR": rr, "KK": kk, "Y2": y2}
            for i in range(NCH + LAGS):
                for name, lag in PE_ORDER:
                    if 0 <= i - lag < NCH:
                        stages[name](i - lag, (i - lag) % 2)


def kernel(x, ctx_2048, **w):
    import numpy as np
    import concourse.bacc as bacc
    from concourse.bass_utils import run_bass_kernel_spmd as run

    w = {name[len("L0_xattn_"):]: np.asarray(a) for name, a in w.items()}
    x, state = np.asarray(x), np.asarray(ctx_2048)

    def halves(a):
        return np.ascontiguousarray(a.reshape(HF, P, -1).transpose(1, 0, 2))

    def dh(a):
        return a.reshape(*a.shape[:-1], H, S).swapaxes(-1, -2).reshape(a.shape)

    by_name = {"ln1_w": w["ln1_w"], "ln1_b": w["ln1_b"], "ln2_w": w["ln2_w"], "ln2_b": w["ln2_b"], "maa_x": w["maa_x"],
               **{f"maa{g}": w["maa_stack"][g] for g in range(5)}, "time_decay": w["time_decay"],
               "u": w["faaaa"].reshape(E), "gn_w": dh(w["gn_w"]), "gn_b": dh(w["gn_b"]),
               "ffn_k": w["ffn_maa_k"], "ffn_r": w["ffn_maa_r"]}
    vecs = np.concatenate([by_name[n].reshape(HF, P).T for n in VECS], axis=1)
    w1 = w["maa_w1"]
    w2 = np.zeros((P, 4 + FOLD, E), np.float32)
    for g in range(4):
        w2[LORA * g:LORA * (g + 1), g] = w["maa_w2"][g]
    for f in range(FOLD):
        w2[LORA * f:LORA * (f + 1), 4 + f] = w["maa_w2"][4]
    dw2 = np.zeros((P, DFOLD, E), np.float32)
    for f in range(DFOLD):
        dw2[DECAY * f:DECAY * (f + 1), f] = w["decay_w2"]
    mats = {"Wr": w["Wr"].T, "Wk": w["Wk"].T, "Wv": dh(w["Wv"].T), "Wg": dh(w["Wg"].T), "Wo": dh(w["Wo"]).T,
            "Fk": w["ffn_Wk"].T, "Fr": w["ffn_Wr"].T, "Fv": w["ffn_Wv"].T}
    large = np.stack([halves(mats[n]) for n in LARGE], axis=1)
    prev = np.stack([halves(state[:, row].T) for row in range(2)], axis=1)
    s0 = halves(state[:, 2:2 + S].reshape(B, E, S).transpose(1, 2, 0).reshape(E, S * B))
    rows = np.arange(P)
    head_mean = (rows[:, None] % H == rows[None, :] % H) / np.float32(S)
    wide = np.stack([(rows[:, None] // S + a * (P // S) == rows[None, :] % H) for a in range(HF)], axis=1)
    narrow = wide[:, :, 0:H]
    consts = np.concatenate([np.eye(P), head_mean, wide.reshape(P, -1), narrow.reshape(P, -1)], axis=1).astype(np.float32)

    arrays = {"x": x.reshape(B * L, E), "prev": prev, "s0": s0.reshape(P, HF, S, B), "vecs": vecs, "w1": halves(w1), "w2": w2,
              "dw1": halves(w["decay_w1"]), "dw2": dw2, "large": large, "consts": consts}
    nc = bacc.Bacc("TRN2", target_bir_lowering=False, num_devices=1)
    args = []
    for name in list(arrays):
        a = np.ascontiguousarray(arrays.pop(name))
        arrays["in_" + name] = a
        args.append(nc.dram_tensor("in_" + name, a.shape, F32, kind="ExternalInput").ap())
    args.append(nc.dram_tensor("out", (B * L, E), F32, kind="ExternalOutput").ap())
    build(nc, *args)
    r = run(nc, [arrays], core_ids=[0])
    return r.results[0]["out"].reshape(B, L, E)
```
